# Optimizing a Trainium2 kernel written in Bass

```python
import numpy as np
import jax
import jax.numpy as jnp

def _softmax(x, axis=-1):
    return jax.nn.softmax(x, axis=axis)

def _gelu(x):
    return jax.nn.gelu(x, approximate=True)

def _silu(x):
    return jax.nn.silu(x)

def _sigmoid(x):
    return jax.nn.sigmoid(x)

def _layernorm(x, axis=-1, eps=1e-05):
    m = jnp.mean(x, axis=axis, keepdims=True)
    v = jnp.var(x, axis=axis, keepdims=True)
    return (x - m) / jnp.sqrt(v + eps)

def _scatter_add(tgt, idx, src, axis=0):
    return tgt.at[idx].add(src)

def _segment_sum(src, seg, n):
    return jax.ops.segment_sum(src, seg, n)
kernel_name = 'mk_cond_seq_d1_seqx_r4_d685b3'

def setup_inputs(seed: int=0):
    np.random.seed(seed)
    _w = jnp.asarray

    def _rec_inputs():
        import jax
        import jax.numpy as jnp
        _rk = jax.random.key(seed)
        x = -0.0003482 + 1 * jax.random.normal(jax.random.fold_in(_rk, 1), (8, 256, 288), jnp.float32)
        _lenS = 256 - jax.random.randint(jax.random.fold_in(_rk, 7), (8,), 0, max(1, 256 // 4) + 1, jnp.int32)
        _lenS2 = 256 - jax.random.randint(jax.random.fold_in(_rk, 8), (8,), 0, max(1, 256 // 4) + 1, jnp.int32)
        cond_1152 = 0.00257642 + 1.0011 * jax.random.normal(jax.random.fold_in(_rk, 11), (8, 288), jnp.float32)
        return (x, cond_1152)
    x, cond_1152 = _rec_inputs()

    def _L0_cond_setup():
        import jax, jax.numpy as jnp
        import numpy as np
        H = 288
        NH = 16
        HD = H // NH
        MLP = int(H * 4.0)
        EPS = 1e-06

        def _ln(z, scale=None):
            m = jnp.mean(z, axis=-1, keepdims=True)
            v = jnp.mean(jnp.square(z - m), axis=-1, keepdims=True)
            y = (z - m) * jax.lax.rsqrt(v + EPS)
            if scale is not None:
                y = y * scale
            return y
        key = jax.random.key(seed)
        ks = jax.random.split(key, 16)
        B, N = (16, 256)
        x = jax.random.normal(ks[0], (B, N, H), dtype=jnp.float32)
        c = jax.random.normal(ks[1], (B, H), dtype=jnp.float32)

        def xav(k, fan_in, fan_out):
            lim = np.sqrt(6.0 / (fan_in + fan_out))
            return jax.random.uniform(k, (fan_in, fan_out), jnp.float32, -lim, lim)
        w_mod = 0.02 * jax.random.normal(ks[2], (H, 6 * H), dtype=jnp.float32)
        b_mod = 0.02 * jax.random.normal(ks[3], (6 * H,), dtype=jnp.float32)
        w_qkv = xav(ks[4], H, 3 * H)
        b_qkv = jnp.zeros((3 * H,), jnp.float32)
        g_q = jnp.ones((HD,), jnp.float32)
        g_k = jnp.ones((HD,), jnp.float32)
        w_proj = xav(ks[5], H, H)
        b_proj = jnp.zeros((H,), jnp.float32)
        w1 = xav(ks[6], H, MLP)
        b1 = jnp.zeros((MLP,), jnp.float32)
        w2 = xav(ks[7], MLP, H)
        b2 = jnp.zeros((H,), jnp.float32)
        return dict(x=x, c=c, w_mod=w_mod, b_mod=b_mod, w_qkv=w_qkv, b_qkv=b_qkv, g_q=g_q, g_k=g_k, w_proj=w_proj, b_proj=b_proj, w1=w1, b1=b1, w2=w2, b2=b2)
    _L0_cond_all = _L0_cond_setup()
    _L0_cond_in = {k: v for k, v in _L0_cond_all.items() if k in ('w_mod', 'b_mod', 'w_qkv', 'b_qkv', 'g_q', 'g_k', 'w_proj', 'b_proj', 'w1', 'b1', 'w2', 'b2')}
    del _L0_cond_all
    return {'x': x, 'cond_1152': cond_1152, 'L0_cond_w_mod': _L0_cond_in['w_mod'], 'L0_cond_b_mod': _L0_cond_in['b_mod'], 'L0_cond_w_qkv': _L0_cond_in['w_qkv'], 'L0_cond_b_qkv': _L0_cond_in['b_qkv'], 'L0_cond_g_q': _L0_cond_in['g_q'], 'L0_cond_g_k': _L0_cond_in['g_k'], 'L0_cond_w_proj': _L0_cond_in['w_proj'], 'L0_cond_b_proj': _L0_cond_in['b_proj'], 'L0_cond_w1': _L0_cond_in['w1'], 'L0_cond_b1': _L0_cond_in['b1'], 'L0_cond_w2': _L0_cond_in['w2'], 'L0_cond_b2': _L0_cond_in['b2']}

def reference(x, cond_1152, L0_cond_w_mod, L0_cond_b_mod, L0_cond_w_qkv, L0_cond_b_qkv, L0_cond_g_q, L0_cond_g_k, L0_cond_w_proj, L0_cond_b_proj, L0_cond_w1, L0_cond_b1, L0_cond_w2, L0_cond_b2):
    import jax
    import jax.numpy as jnp

    def _L0_cond_ref(x, c, w_mod, b_mod, w_qkv, b_qkv, g_q, g_k, w_proj, b_proj, w1, b1, w2, b2):
        import jax, jax.numpy as jnp
        import numpy as np
        H = 288
        NH = 16
        HD = H // NH
        MLP = int(H * 4.0)
        EPS = 1e-06

        def _ln(z, scale=None):
            m = jnp.mean(z, axis=-1, keepdims=True)
            v = jnp.mean(jnp.square(z - m), axis=-1, keepdims=True)
            y = (z - m) * jax.lax.rsqrt(v + EPS)
            if scale is not None:
                y = y * scale
            return y
        B, N, _ = x.shape
        mod = jax.nn.swish(c) @ w_mod + b_mod
        sh_msa, sc_msa, g_msa, sh_mlp, sc_mlp, g_mlp = jnp.split(mod, 6, axis=1)
        xn = _ln(x) * (1 + sc_msa[:, None, :]) + sh_msa[:, None, :]
        qkv = xn @ w_qkv + b_qkv
        qkv = qkv.reshape(B, N, 3, NH, HD).transpose(2, 0, 3, 1, 4)
        q, k, v = (qkv[0], qkv[1], qkv[2])
        q = _ln(q, g_q)
        k = _ln(k, g_k)
        attn = jax.nn.softmax(jnp.einsum('bhqd,bhkd->bhqk', q, k) * HD ** (-0.5), axis=-1)
        o = jnp.einsum('bhqk,bhkd->bhqd', attn, v)
        o = o.transpose(0, 2, 1, 3).reshape(B, N, H) @ w_proj + b_proj
        x = x + g_msa[:, None, :] * o
        xn2 = _ln(x) * (1 + sc_mlp[:, None, :]) + sh_mlp[:, None, :]
        h = jax.nn.gelu(xn2 @ w1 + b1, approximate=True)
        x = x + g_mlp[:, None, :] * (h @ w2 + b2)
        return x
    x = _L0_cond_ref(x, cond_1152, L0_cond_w_mod, L0_cond_b_mod, L0_cond_w_qkv, L0_cond_b_qkv, L0_cond_g_q, L0_cond_g_k, L0_cond_w_proj, L0_cond_b_proj, L0_cond_w1, L0_cond_b1, L0_cond_w2, L0_cond_b2)
    return x

_drawn_inputs = setup_inputs


def setup_inputs(seed=0):
    import zlib

    import numpy as np

    out = dict(_drawn_inputs(seed))
    spreads = {'L0_cond_b_qkv': (0.0, 0.392),
     'L0_cond_g_q': (1.0, 0.6),
     'L0_cond_g_k': (1.0, 0.6),
     'L0_cond_b_proj': (0.0, 0.399),
     'L0_cond_b1': (0.0, 0.519),
     'L0_cond_b2': (0.0, 0.429)}
    factors = {'L0_cond_b_mod': 5.117}
    for name, (base, spread) in spreads.items():
        noise = np.random.default_rng([zlib.crc32(name.encode()), seed]).standard_normal(out[name].shape)
        drawn = base * np.exp(spread * noise) if base else spread * noise
        out[name] = jnp.asarray(drawn.astype(out[name].dtype))
    for name, factor in factors.items():
        out[name] = (out[name] * factor).astype(out[name].dtype)
    return out
```

```python
from contextlib import ExitStack

import concourse.bass as bass
from concourse import mybir

F32 = mybir.dt.float32
F32R = mybir.dt.float32r
I32 = mybir.dt.int32
ACT = mybir.ActivationFunctionType
ALU = mybir.AluOpType
AX = mybir.AxisListType

P = 128
SEQS, SEQ, H = 8, 256, 288
NH = 16
HD = H // NH
MLP = 4 * H
TILES = SEQ // P
UNITS = NH // 2
GROUPS = NH // 4
FT = MLP // P
MU = (FT + 1) // 2
TAIL = H - 2 * P
TAIL3 = 3 * TAIL
STACK = TAIL3 + 2
ZW = 2 * P + TAIL3
OW = ZW + 2 * P
KM = H // 3
HALF = 64
SHIFT = 3 * HD
SROWS = SHIFT + 1
VW = 32
NMOD = 6 * H
EPS = 1e-6
SCORE_BOUND = 60.0
W_QKV, W_PROJ, W_1 = 0, 3 * H, 4 * H
W_ALL = 4 * H + MLP
QK = 2 * H


def dit_block(nc, x, condT, w_mod, b_mod, w_qkv, b_qkv, g_q, g_k, w_proj, b_proj, w1, b1, w2, b2,
              gate_scratch, out):
    x_seqs = x.rearrange("s (t p) f -> s p t f", p=P)
    out_seqs = out.rearrange("s (t p) f -> s p t f", p=P)

    with ExitStack() as ctx:
        def sb(name, shape, dt=F32):
            return ctx.enter_context(nc.sbuf_tensor(name, shape, dt))

        def sem(name):
            return ctx.enter_context(nc.semaphore(name))

        w_hi = sb("w_hi", [P, 2, W_ALL], F32R)
        w_lo = sb("w_lo", [P, 2, W_ALL], F32R)
        w_tail = sb("w_tail", [STACK, W_ALL], F32R)
        w2_hi = sb("w2_hi", [P, FT, H], F32R)
        w2_lo = sb("w2_lo", [P, FT, H], F32R)
        b2_rows = sb("b2_rows", [P, H], F32R)
        arena = sb("arena", [P, 3 * W_ALL + 3 * NMOD + FT * H])
        raw_w = arena[:, 0:3 * W_ALL].rearrange("p (k n) -> p k n", k=3)
        raw_mod = arena[:, 3 * W_ALL:3 * W_ALL + 3 * NMOD].rearrange("p (k n) -> p k n", k=3)
        raw_w2 = arena[:, 3 * W_ALL + 3 * NMOD:].rearrange("p (k n) -> p k n", k=FT)

        def carve(start, *shape):
            size = shape[0] * shape[1]
            return arena[:, start:start + size].rearrange("p (u n) -> p u n", u=shape[0]), start + size

        at = 0
        prob, at = carve(at, 4, 4 * SEQ)
        o_norm, at = carve(at, TILES, H)
        xv_mlp, at = carve(at, 3, SEQ)
        attn, at = carve(at, GROUPS, SEQ)
        assert at <= 3 * W_ALL
        at = 3 * W_ALL
        squares, at = carve(at, 2, QK)
        qk_norm, at = carve(at, 2, QK)
        q_gained, at = carve(at, 2, H)
        hidden, at = carve(at, 2, 2 * SEQ)
        assert at <= 3 * W_ALL + 3 * NMOD
        at = 3 * W_ALL + 3 * NMOD
        y, at = carve(at, TILES, H)
        x2_prev, at = carve(at, TILES, H)
        x2, at = carve(at, TILES, H)
        x_res, at = carve(at, TILES, H)
        gate1, at = carve(at, 1, H)
        assert at <= 3 * W_ALL + 3 * NMOD + FT * H
        x_ln = sb("x_ln", [P, TILES, H])
        z = sb("z", [P, TILES, ZW])
        xv_qkv = sb("xv_qkv", [P, 3, SEQ])
        gate2 = sb("gate2", [P, H])
        xs_hi = [sb(f"xs_hi_{n}", [P, 2, SEQ], F32R) for n in ("qkv", "mlp")]
        xs_lo = [sb(f"xs_lo_{n}", [P, 2, SEQ], F32R) for n in ("qkv", "mlp")]
        xs_tail = [sb(f"xs_tail_{n}", [STACK, SEQ], F32R) for n in ("qkv", "mlp")]
        o_split = sb("o_split", [P, TILES, OW], F32R)
        o_stack = sb("o_stack", [P, TILES, 4 * P], F32R)
        o_tail = sb("o_tail", [STACK, SEQ], F32R)
        qk_stack = sb("qk_stack", [P, TILES, 2, NH, HALF], F32R)
        qT = sb("qT", [P, UNITS, SEQ], F32R)
        kT = sb("kT", [P, UNITS, SEQ], F32R)
        v_ext = sb("v_ext", [P, TILES, NH, VW])
        hid_hi = sb("hid_hi", [P, 2, 2 * SEQ], F32R)
        hid_lo = sb("hid_lo", [P, 2, 2 * SEQ], F32R)
        ident = sb("ident", [P, P])
        ident_r = sb("ident_r", [P, P], F32R)
        ones_r = sb("ones_r", [P, P], F32R)
        cond = sb("cond", [KM, 3, SEQS])
        cond_tanh = sb("cond_tanh", [KM, 3, SEQS])
        silu = sb("silu", [KM + 1, 3, SEQS])
        mod_all = sb("mod_all", [P, 4, 3, SEQS])
        mod_cur = [sb(f"mod_cur_{n}", [P, 2, 3]) for n in ("qkv", "mlp")]
        gate_rows = sb("gate_rows", [SEQS, 2, H])
        col_mean = sb("col_mean", [P, 3, 2 * NH])
        g_both = sb("g_both", [P, 2, HD])
        gain = sb("gain", [P, HD])
        bound = sb("bound", [P, 1])
        flag = sb("flag", [P, 1], I32)
        minus_half = sb("minus_half", [P, 2 * NH])
        ln_stats = sb("ln_stats", [P, TILES, 6])
        ln_mv = sb("ln_mv", [P, TILES, 2])
        ln_var = sb("ln_var", [P, TILES])
        ln_rstd = sb("ln_rstd", [P, TILES])
        qk_sum = sb("qk_sum", [P, 2 * NH])
        qk_var = sb("qk_var", [P, 2 * NH])
        qk_rstd = sb("qk_rstd", [P, 2 * NH])
        o_recip = sb("o_recip", [P, NH])
        neg_max = sb("neg_max", [P, TILES, NH])
        shiftT = sb("shiftT", [NH, SEQ])

        psum = ctx.enter_context(nc.psum_tensor("psum", [P, 8, 512], F32))
        hidden_bank = (2, 5)

        s_const = sem("constants_made")
        s_ident0, s_ident = sem("identity_zeroed"), sem("identity_ready")
        s_cond, s_g = sem("cond_loaded"), sem("gains_loaded")
        s_modraw, s_qkvraw, s_wraw, s_w2raw = sem("w_mod_loaded"), sem("w_qkv_loaded"), sem("w_proj_w1_loaded"), sem("w2_loaded")
        s_setup, s_pstep = sem("vector_setup_step"), sem("pool_setup_step")
        s_wqkv, s_wrest = sem("w_qkv_split"), sem("other_weights_split")
        s_tanh, s_silu = sem("tanh_done"), sem("silu_ready")
        s_modmm, s_gatemm = sem("mod_products_done"), sem("gate_products_done")
        s_mod, s_gate, s_stored = sem("mod_columns_ready"), sem("gate_rows_ready"), sem("gate_rows_stored")
        s_gain, s_flag = sem("gain_ready"), sem("flag_ready")
        s_x, s_xres, s_g1, s_g2 = sem("x_loaded"), sem("x_res_loaded"), sem("gate1_loaded"), sem("gate2_loaded")
        both = ("qkv", "mlp")
        s_stats = [sem(f"ln_stats_{n}") for n in both]
        s_aggr = [sem(f"ln_aggregated_{n}") for n in both]
        s_var = [sem(f"ln_variance_{n}") for n in both]
        s_rstd = [sem(f"ln_rstd_{n}") for n in both]
        s_z = [sem(f"z_ready_{n}") for n in both]
        s_modc = [sem(f"mod_copied_{n}") for n in both]
        s_zT = [sem(f"z_transposed_{n}") for n in both]
        s_xv = [sem(f"x_modulated_{n}") for n in both]
        s_round = [sem(f"x_rounded_{n}") for n in both]
        s_xs = [sem(f"x_split_{n}") for n in both]
        s_qkv = sem("qkv_done")
        s_sq, s_v = sem("squares_done"), sem("v_read")
        s_qsum, s_qvar, s_qrstd = sem("square_sums_done"), sem("qk_variance"), sem("qk_rstd_ready")
        s_qkn, s_qg = sem("qk_normalised"), sem("q_gained_ready")
        s_qround, s_stack = sem("qk_rounded"), sem("qk_stack_ready")
        s_st, s_stq, s_stk = sem("stack_tile_done"), sem("q_stack_transposed"), sem("k_stack_transposed")
        s_qT, s_kT = sem("qT_written"), sem("kT_written")
        s_score, s_exp = sem("scores_done"), sem("exp_done")
        s_pv, s_attn = sem("attn_group_done"), sem("attn_group_read")
        s_oT, s_recip, s_on = sem("attn_transposed"), sem("row_sums_inverted"), sem("o_normalised")
        s_oround, s_os = sem("o_rounded"), sem("o_split_ready")
        s_oback, s_ostack = sem("o_transposed"), sem("o_stack_written")
        s_proj, s_pg, s_x2 = sem("proj_done"), sem("proj_gated"), sem("x2_ready")
        s_x2c = sem("x2_handed_on")
        s_up, s_gelu = sem("mlp_up_done"), sem("gelu_done")
        s_hround, s_hs, s_down = sem("hidden_rounded"), sem("hidden_split"), sem("mlp_down_done")
        s_yg, s_y, s_out = sem("mlp_gated"), sem("y_ready"), sem("y_stored")
        s_ms, s_mx = sem("shift_scores_done"), sem("shift_maxima_done")
        s_mT, s_mc, s_md = sem("maxima_transposed"), sem("maxima_copied"), sem("shift_rows_written")

        block = ctx.enter_context(nc.Block())

        def passes(engine, body):
            body(0, True, False)
            body(1, True, True)
            with engine.Fori(2, SEQS - 1) as p:
                body(p, True, True)
            body(SEQS - 1, False, True)

        def dense(pe, dst, hi, lo, tail, cols, act_moves):
            terms = [(hi(0), w_hi[:, 0, cols]), (hi(1), w_hi[:, 1, cols]),
                     (hi(0), w_lo[:, 0, cols]), (hi(1), w_lo[:, 1, cols]),
                     (lo(0), w_hi[:, 0, cols]), (lo(1), w_hi[:, 1, cols]),
                     (tail, w_tail[:, cols])]
            for n, (a, w) in enumerate(terms):
                lhsT, rhs = (w, a) if act_moves else (a, w)
                last = nc.tensor.matmul(dst, lhsT, rhs, start=(n == 0), stop=(n == len(terms) - 1))
            return last

        @block.sync
        def _(sp):
            def row(v):
                return v.rearrange("(o n) -> o n", o=1)

            sp.dma_start(cond[:, :, :], condT.rearrange("(k p) b -> p k b", p=KM)).then_inc(s_cond, 16)
            for i, g in enumerate((g_q, g_k)):
                sp.dma_start(g_both[:, i, :], row(g).broadcast_to((P, HD))).then_inc(s_g, 16)
            sp.dma_start(x_ln[:, :, :], x_seqs[0]).then_inc(s_x, 16)
            sp.dma_start(raw_mod[0:KM, :, :], w_mod.rearrange("(k p) n -> p k n", p=KM)).then_inc(s_modraw, 16)
            sp.dma_start(raw_mod[KM:KM + 1, 2, :], row(b_mod)).then_inc(s_modraw, 16)
            for w, b, c, s in ((w_qkv, b_qkv, W_QKV, s_qkvraw), (w_proj, b_proj, W_PROJ, s_wraw), (w1, b1, W_1, s_wraw)):
                n = w.shape[1]
                sp.dma_start(raw_w[:, 0:2, c:c + n], w[0:2 * P, :].rearrange("(k p) n -> p k n", p=P)).then_inc(s, 16)
                for r in range(3):
                    sp.dma_start(raw_w[r * TAIL:(r + 1) * TAIL, 2, c:c + n], w[2 * P:H, :]).then_inc(s, 16)
                for r in range(2):
                    sp.dma_start(raw_w[TAIL3 + r:TAIL3 + r + 1, 2, c:c + n], row(b)).then_inc(s, 16)
            sp.dma_start(raw_w2, w2.rearrange("(k p) n -> p k n", p=P)).then_inc(s_w2raw, 16)
            for r in range(2):
                sp.dma_start(gate2[r:r + 1, :], row(b2)).then_inc(s_w2raw, 16)
            sp.wait_ge(s_gate, 1)
            sp.dma_start(gate_scratch, gate_rows[:, :, :].rearrange("b g f -> b (g f)")).then_inc(s_stored, 16)
            sp.wait_ge(s_stored, 16)
            sp.wait_ge(s_flag, 1)
            needs_shift = sp.value_load(flag[0:1, 0:1], min_val=0, max_val=1)
            sp.wait_ge(s_wrest, 3)

            def body(p, more, prev):
                with sp.If(needs_shift > 0):
                    sp.wait_ge(s_mc, p + 1)
                    for j in range(2):
                        at_row = HALF * j + SHIFT
                        sp.dma_start(qT[at_row:at_row + 1, :, :].bitcast(F32),
                                     shiftT[UNITS * j:UNITS * (j + 1), :]).then_inc(s_md, 16)
                if more:
                    sp.wait_ge(s_z[0], p + 1)
                    sp.dma_start(x_ln[:, :, :], x_seqs[p + 1]).then_inc(s_x, 16)
                sp.wait_ge(s_x2, p * TILES)
                sp.dma_start(x_res[:, :, :], x_seqs[p]).then_inc(s_xres, 16)
                sp.wait_ge(s_pg, p * TILES)
                sp.dma_start(gate1[:, 0, :], gate_scratch[bass.ds(p, 1), 0:H].broadcast_to((P, H))).then_inc(s_g1, 16)
                if prev:
                    mlp_io(p - 1)

            def mlp_io(m):
                sp.wait_ge(s_yg, m * TILES)
                sp.dma_start(gate2[:, :], gate_scratch[bass.ds(m, 1), H:2 * H].broadcast_to((P, H))).then_inc(s_g2, 16)
                sp.wait_ge(s_y, m * TILES + TILES)
                sp.dma_start(out_seqs[m], y[:, :, :]).then_inc(s_out, 16)

            passes(sp, body)
            mlp_io(SEQS - 1)
            sp.wait_ge(s_out, 16 * SEQS)

        @block.gpsimd
        def _(pool):
            nc.gpsimd.memset(ident[:, :], 0.0).then_inc(s_ident0, 1)
            nc.gpsimd.memset(minus_half[:, :], -0.5).then_inc(s_const, 1)
            pool.wait_ge(s_ident0, 1)
            nc.gpsimd.affine_select(out=ident[:, :], in_=ident[:, :], compare_op=ALU.not_equal, fill=1.0, base=0,
                                    pattern=[[-1, P]], channel_multiplier=1).then_inc(s_ident, 1)

            def power(s_in, s_result, dst, src, n):
                pool.wait_ge(s_in, n)
                nc.gpsimd.tensor_tensor(dst, src, minus_half[:, 0:src.shape[1]], ALU.pow).then_inc(s_result, 1)

            def ln_power(which, n):
                power(s_var[which], s_rstd[which], ln_rstd[:, :], ln_var[:, :], n + 1)

            def copy_mod(which, n):
                pool.wait_ge(s_mod, 1)
                pool.wait_ge(s_xv[which], 3 * n)
                nc.gpsimd.tensor_copy(mod_cur[which][:, :, :], mod_all[:, 2 * which:2 * which + 2, :, n]).then_inc(s_modc[which], 1)

            def qk_gain(q, t):
                n = q * TILES + t
                power(s_qvar, s_qrstd, qk_rstd[:, :], qk_var[:, :], n + 1)
                pool.wait_ge(s_qkn, n + 1)
                nc.gpsimd.tensor_tensor(
                    q_gained[:, t, :].rearrange("p (h d) -> p h d", d=HD),
                    qk_norm[:, t, 0:H].rearrange("p (h d) -> p h d", d=HD),
                    gain[:, :].rearrange("p (o d) -> p o d", o=1).broadcast_to((P, NH, HD)), ALU.mult).then_inc(s_qg, 1)

            pool.wait_ge(s_const, 2)
            ln_power(0, 0)
            copy_mod(0, 0)
            pool.wait_ge(s_gain, 1)
            qk_gain(0, 0)
            qk_gain(0, 1)

            done = 0

            def step(ins):
                nonlocal done
                done += 1
                ins.then_inc(s_pstep, 1)

            pool.wait_ge(s_wraw, 16 * 12)
            for c, n in ((W_PROJ, H), (W_1, MLP)):
                cols = slice(c, c + n)
                step(nc.gpsimd.tensor_copy(w_tail[:, cols], raw_w[0:STACK, 2, cols]))
                for k in range(2):
                    step(nc.gpsimd.tensor_copy(w_hi[:, k, cols], raw_w[:, k, cols]))
                pool.wait_ge(s_pstep, done)
                step(nc.gpsimd.tensor_tensor(w_tail[2 * TAIL:STACK, cols], raw_w[2 * TAIL:STACK, 2, cols],
                                             w_tail[2 * TAIL:STACK, cols], ALU.subtract))
                pool.wait_ge(s_pstep, done)
                for k in range(2):
                    step(nc.gpsimd.tensor_tensor(w_lo[:, k, cols], raw_w[:, k, cols], w_hi[:, k, cols], ALU.subtract))
                pool.wait_ge(s_pstep, done)
                step(nc.gpsimd.tensor_copy(w_tail[TAIL3:TAIL3 + 1, cols], raw_w[TAIL3:TAIL3 + 1, 2, cols]))
                pool.wait_ge(s_pstep, done)
                pool.sem_inc(s_wrest, 1)
            pool.wait_ge(s_w2raw, 48)
            step(nc.gpsimd.tensor_copy(b2_rows[0:2, :], gate2[0:2, :]))
            step(nc.gpsimd.tensor_copy(w2_hi[:, :, :], raw_w2))
            pool.wait_ge(s_pstep, done)
            step(nc.gpsimd.tensor_tensor(w2_lo[:, :, :], raw_w2, w2_hi[:, :, :], ALU.subtract))
            step(nc.gpsimd.tensor_tensor(b2_rows[0:2, :], gate2[0:2, :], b2_rows[0:2, :], ALU.subtract))
            pool.wait_ge(s_pstep, done)
            step(nc.gpsimd.tensor_copy(b2_rows[0:1, :], gate2[0:1, :]))
            pool.wait_ge(s_pstep, done)
            pool.sem_inc(s_wrest, 1)

            def body(p, more, prev):
                if more:
                    ln_power(0, p + 1)
                    copy_mod(0, p + 1)
                    qk_gain(p + 1, 0)
                    qk_gain(p + 1, 1)
                ln_power(1, p)
                copy_mod(1, p)

            passes(pool, body)

        @block.tensor
        def _(pe):
            pe.wait_ge(s_silu, 1)
            pe.wait_ge(s_modraw, 32)
            def mod_product(dst, lhs, rhs):
                for k in range(3):
                    rows = KM + (k == 2)
                    last = nc.tensor.matmul(dst, lhs(k, rows), rhs(k, rows), start=(k == 0), stop=(k == 2))
                return last

            for i, kind in enumerate((0, 1, 3, 4)):
                for j in range(3):
                    parts = [(0, P, j * P)] if j < 2 else [(r * TAIL, TAIL, 2 * P) for r in range(3)]
                    for row0, m, col0 in parts:
                        at = (3 * i + j) * SEQS
                        last = mod_product(psum[row0:row0 + m, 7, at:at + SEQS],
                                           lambda k, rows: raw_mod[0:rows, k, kind * H + col0:kind * H + col0 + m],
                                           lambda k, rows: silu[0:rows, k, :])
            last.then_inc(s_modmm, 1)
            for i, kind in enumerate((2, 5)):
                last = mod_product(psum[0:SEQS, 4 + i, 0:H], lambda k, rows: silu[0:rows, k, :],
                                   lambda k, rows: raw_mod[0:rows, k, kind * H:(kind + 1) * H])
            last.then_inc(s_gatemm, 1)

            def ln_transpose(which, n, j):
                pe.wait_ge(s_z[which], n + 1)
                rows = P if j < 2 else TAIL3
                for t in range(TILES):
                    last = nc.tensor.transpose(psum[0:rows, 6 + j % 2, t * P:(t + 1) * P],
                                               z[:, t, j * P:j * P + rows], ident[:, :])
                last.then_inc(s_zT[which], 1)

            def qkv(q, t):
                pe.wait_ge(s_xs[0], 3 * q + 3)
                tok = slice(t * P, (t + 1) * P)
                for c in range(3):
                    last = dense(pe, psum[:, 3 * t + c, 0:H], lambda k: xs_hi[0][:, k, tok],
                                 lambda k: xs_lo[0][:, k, tok], xs_tail[0][:, tok],
                                 slice(W_QKV + c * H, W_QKV + (c + 1) * H), False)
                last.then_inc(s_qkv, 1)

            def stack_transpose(q, t, first):
                pe.wait_ge(s_stack, q * TILES + t + 1)
                for i in range(2):
                    n = 2 * t + i
                    for c, s_done, s_read in ((0, s_stq, s_qT), (1, s_stk, s_kT)):
                        if not (first and n == 0):
                            pe.wait_ge(s_read, 4 * q + n)
                        for k in range(4):
                            u = 4 * i + k
                            last = nc.tensor.matmul(
                                psum[:, 6 + c, k * P:(k + 1) * P],
                                qk_stack[:, t, c, 2 * u:2 * u + 2, :].rearrange("p h r -> p (h r)"),
                                ident_r[:, :], start=True, stop=True)
                        last.then_inc(s_done, 1)

            def scores(p, u):
                if u >= 2:
                    pe.wait_ge(s_exp, UNITS * p + u - 1)
                two = 2 * (u % 2)
                for kt in range(TILES):
                    for j in range(2):
                        rows = slice(HALF * j, HALF * j + SROWS)
                        last = nc.tensor.matmul(psum[:, two + j, kt * SEQ:(kt + 1) * SEQ],
                                                kT[rows, u, kt * P:(kt + 1) * P], qT[rows, u, :],
                                                start=True, stop=True)
                last.then_inc(s_score, 1)

            def values(p, g):
                pe.wait_ge(s_exp, UNITS * p + 2 * g + 2)
                if g >= 2:
                    pe.wait_ge(s_attn, GROUPS * p + g - 1)
                for kt in range(TILES):
                    for c in range(4):
                        u, j = 2 * g + c // 2, c % 2
                        last = nc.tensor.matmul(
                            psum[32 * c:32 * c + 32, 4 + g % 2, 0:SEQ], v_ext[:, kt, 4 * g + c, :],
                            prob[:, u % 4, j * 2 * SEQ + kt * SEQ:j * 2 * SEQ + (kt + 1) * SEQ],
                            start=(kt == 0), stop=(kt == TILES - 1))
                last.then_inc(s_pv, 1)

            def o_back(p, t):
                pe.wait_ge(s_os, p * TILES + t + 1)
                if t == 0:
                    pe.wait_ge(s_on, p * TILES + TILES)
                else:
                    pe.wait_ge(s_ostack, 4 * p + 2 * t)
                for i, c in enumerate((0, P, ZW, ZW + P)):
                    nc.tensor.matmul(psum[:, 6, i * P:(i + 1) * P], o_split[:, t, c:c + P], ident_r[:, :],
                                     start=True, stop=True)
                nc.tensor.matmul(psum[0:TAIL3, 7, 0:P], o_split[:, t, 2 * P:ZW], ident_r[:, :],
                                 start=True, stop=True).then_inc(s_oback, 1)

            def project(p, t):
                pe.wait_ge(s_ostack, 4 * p + 4)
                dense(pe, psum[:, 6 + t, 0:H], lambda k: o_stack[:, t, k * P:(k + 1) * P],
                      lambda k: o_stack[:, t, (2 + k) * P:(3 + k) * P], o_tail[:, t * P:(t + 1) * P],
                      slice(W_PROJ, W_PROJ + H), False).then_inc(s_proj, 1)

            def unit_tiles(i):
                return range(2 * i, min(2 * i + 2, FT))

            def up(m, i):
                if i >= 2:
                    pe.wait_ge(s_gelu, MU * m + i - 1)
                for f in unit_tiles(i):
                    last = dense(pe, psum[:, hidden_bank[i % 2], (f % 2) * SEQ:(f % 2 + 1) * SEQ],
                                 lambda k: xs_hi[1][:, k, :], lambda k: xs_lo[1][:, k, :], xs_tail[1][:, :],
                                 slice(W_1 + f * P, W_1 + (f + 1) * P), True)
                last.then_inc(s_up, 1)

            def down(m, i):
                pe.wait_ge(s_hs, MU * m + i + 1)
                for t in range(TILES):
                    if i == 0:
                        nc.tensor.matmul(psum[:, t, 0:H], ones_r[:, :], b2_rows[:, :], start=True, stop=False)
                    for f in unit_tiles(i):
                        tok = slice((f % 2) * SEQ + t * P, (f % 2) * SEQ + (t + 1) * P)
                        for n, (a, w) in enumerate(((hid_hi, w2_hi), (hid_hi, w2_lo), (hid_lo, w2_hi))):
                            last = nc.tensor.matmul(psum[:, t, 0:H], a[:, i % 2, tok], w[:, f, :],
                                                    start=False, stop=(f == FT - 1 and n == 2))
                last.then_inc(s_down, 1)

            def mlp(m, after_qkv):
                pe.wait_ge(s_xs[1], 3 * m + 3)
                if after_qkv:
                    pe.wait_ge(s_v, (m + 2) * TILES + TILES)
                up(m, 0)
                up(m, 1)
                if after_qkv:
                    pe.wait_ge(s_qkn, (m + 2) * TILES + TILES)
                for i in range(MU):
                    down(m, i)
                    if i + 2 < MU:
                        up(m, i + 2)

            pe.wait_ge(s_mod, 1)
            pe.wait_ge(s_ident, 1)
            ln_transpose(0, 0, 0)
            ln_transpose(0, 0, 1)
            pe.wait_ge(s_xv[0], 1)
            ln_transpose(0, 0, 2)
            pe.wait_ge(s_wqkv, 1)
            pe.wait_ge(s_gate, 1)
            qkv(0, 0)
            qkv(0, 1)
            pe.wait_ge(s_xv[0], 3)
            pe.wait_ge(s_const, 2)
            stack_transpose(0, 0, True)
            stack_transpose(0, 1, True)
            pe.wait_ge(s_flag, 1)
            needs_shift = pe.value_load(flag[0:1, 0:1], min_val=0, max_val=1)

            def body(p, more, prev):
                pe.wait_ge(s_qT, 4 * p + 4)
                pe.wait_ge(s_kT, 4 * p + 4)
                pe.wait_ge(s_v, p * TILES + TILES)
                pe.wait_ge(s_qkn, p * TILES + TILES)
                if prev:
                    pe.wait_ge(s_yg, (p - 1) * TILES)
                    pe.wait_ge(s_gelu, (p - 1) * MU)
                with pe.If(needs_shift > 0):
                    for n in range(TILES * GROUPS):
                        t, g = n // GROUPS, n % GROUPS
                        if n >= 2:
                            pe.wait_ge(s_mx, TILES * GROUPS * p + n - 1)
                        for c in range(4):
                            u, j = 2 * g + c // 2, c % 2
                            rows = slice(HALF * j, HALF * j + SHIFT)
                            last = nc.tensor.matmul(psum[:, 2 * (n % 2) + j, (c // 2) * SEQ:(c // 2 + 1) * SEQ],
                                                    qT[rows, u, t * P:(t + 1) * P], kT[rows, u, :],
                                                    start=True, stop=True)
                        last.then_inc(s_ms, 1)
                    pe.wait_ge(s_mx, TILES * GROUPS * (p + 1))
                    for t in range(TILES):
                        last = nc.tensor.transpose(psum[0:NH, 4, t * P:(t + 1) * P], neg_max[:, t, :], ident[:, :])
                    last.then_inc(s_mT, 1)
                    pe.wait_ge(s_md, 32 * (p + 1))
                scores(p, 0)
                scores(p, 1)
                for g in range(GROUPS):
                    if g < GROUPS - 1:
                        scores(p, 2 * g + 2)
                        scores(p, 2 * g + 3)
                    values(p, g)
                    if more and g == 1:
                        pe.wait_ge(s_xv[1], 3 * p)
                        ln_transpose(0, p + 1, 0)
                        ln_transpose(0, p + 1, 1)
                    if more and g == 2:
                        pe.wait_ge(s_xv[0], 3 * p + 4)
                        ln_transpose(0, p + 1, 2)
                if more:
                    pe.wait_ge(s_xv[0], 3 * p + 6)
                else:
                    pe.wait_ge(s_xv[1], 3 * p)
                pe.wait_ge(s_attn, GROUPS * p + GROUPS)
                for t in range(TILES):
                    for g in range(GROUPS):
                        last = nc.tensor.transpose(psum[:, 6 + t, g * P:(g + 1) * P],
                                                   attn[:, g, t * P:(t + 1) * P], ident[:, :])
                    last.then_inc(s_oT, 1)
                if more:
                    pe.wait_ge(s_exp, UNITS * p + UNITS)
                    qkv(p + 1, 0)
                if not prev:
                    pe.wait_ge(s_wrest, 1)
                o_back(p, 0)
                if more:
                    qkv(p + 1, 1)
                o_back(p, 1)
                project(p, 0)
                project(p, 1)
                if prev:
                    mlp(p - 1, more)
                if more:
                    pe.wait_ge(s_pg, p * TILES + TILES)
                    stack_transpose(p + 1, 0, True)
                    stack_transpose(p + 1, 1, True)
                    pe.wait_ge(s_qT, 4 * p + 8)
                    pe.wait_ge(s_kT, 4 * p + 8)
                else:
                    pe.wait_ge(s_pg, p * TILES + TILES)
                ln_transpose(1, p, 0)
                ln_transpose(1, p, 1)
                pe.wait_ge(s_xv[1], 3 * p + 1)
                ln_transpose(1, p, 2)
                if not prev:
                    pe.wait_ge(s_wrest, 3)

            passes(pe, body)
            pe.wait_ge(s_yg, (SEQS - 1) * TILES)
            mlp(SEQS - 1, False)

        @block.scalar
        def _(act):
            act.wait_ge(s_cond, 16)
            nc.scalar.activation(cond_tanh[:, :, :], cond[:, :, :], ACT.Tanh, scale=0.5).then_inc(s_tanh, 1)

            def modulate(which, n, j):
                xv = (xv_qkv, xv_mlp)[which]
                rows = P if j < 2 else TAIL3
                act.wait_ge(s_zT[which], 3 * n + j + 1)
                act.wait_ge(s_modc[which], n + 1)
                act.wait_ge(s_xs[which], 3 * n)
                nc.scalar.activation(xv[0:rows, j, :], psum[0:rows, 6 + j % 2, 0:SEQ], ACT.Identity,
                                     bias=mod_cur[which][0:rows, 0, j:j + 1],
                                     scale=mod_cur[which][0:rows, 1, j:j + 1]).then_inc(s_xv[which], 1)

            def qkv_read(q, t):
                act.wait_ge(s_qkv, q * TILES + t + 1)
                act.wait_ge(s_qsum, q * TILES)
                nc.scalar.activation(squares[:, t, :].rearrange("p (c n) -> p c n", c=2),
                                     psum[:, 3 * t:3 * t + 2, 0:H], ACT.Square).then_inc(s_sq, 1)
                act.wait_ge(s_pv, q * GROUPS)
                nc.scalar.activation(v_ext[:, t, :, 0:HD], psum[:, 3 * t + 2, 0:H].rearrange("p (h d) -> p h d", d=HD),
                                     ACT.Copy).then_inc(s_v, 1)

            def q_read(q, t):
                for i in range(2):
                    act.wait_ge(s_stq, 4 * q + 2 * t + i + 1)
                    act.wait_ge(s_score, UNITS * q)
                    nc.scalar.activation(qT[:, 4 * i:4 * i + 4, t * P:(t + 1) * P],
                                         psum[:, 6, :].rearrange("p (u n) -> p u n", u=4), ACT.Copy).then_inc(s_qT, 1)

            def exp(p, u):
                act.wait_ge(s_score, UNITS * p + u + 1)
                act.wait_ge(s_pv, GROUPS * p + u // 2 - 1 if u >= 4 else GROUPS * p)
                nc.scalar.activation(prob[:, u % 4, :].rearrange("p (c n) -> p c n", c=2),
                                     psum[:, 2 * (u % 2):2 * (u % 2) + 2, :], ACT.Exp).then_inc(s_exp, 1)

            def o_read(p, t):
                act.wait_ge(s_oback, p * TILES + t + 1)
                act.wait_ge(s_proj, p * TILES)
                nc.scalar.activation(o_stack[:, t, :], psum[:, 6, :], ACT.Copy).then_inc(s_ostack, 1)
                nc.scalar.activation(o_tail[0:TAIL3, t * P:(t + 1) * P], psum[0:TAIL3, 7, 0:P], ACT.Copy).then_inc(s_ostack, 1)

            def gelu(m, i):
                n = SEQ * len(range(2 * i, min(2 * i + 2, FT)))
                act.wait_ge(s_up, MU * m + i + 1)
                act.wait_ge(s_hs, MU * m + i - 1 if i >= 2 else MU * m)
                nc.scalar.activation(hidden[:, i % 2, 0:n], psum[:, hidden_bank[i % 2], 0:n],
                                     ACT.Gelu_apprx_tanh).then_inc(s_gelu, 1)

            for j in range(3):
                modulate(0, 0, j)
            act.wait_ge(s_const, 2)
            qkv_read(0, 0)
            qkv_read(0, 1)
            q_read(0, 0)
            q_read(0, 1)
            act.wait_ge(s_wrest, 3)

            def body(p, more, prev):
                for u in range(UNITS):
                    exp(p, u)
                    if more and u == 5:
                        modulate(0, p + 1, 0)
                        modulate(0, p + 1, 1)
                if more:
                    modulate(0, p + 1, 2)
                    qkv_read(p + 1, 0)
                o_read(p, 0)
                if more:
                    qkv_read(p + 1, 1)
                o_read(p, 1)
                if prev:
                    for i in range(MU):
                        gelu(p - 1, i)
                if more:
                    q_read(p + 1, 0)
                    q_read(p + 1, 1)
                for j in range(3):
                    modulate(1, p, j)

            passes(act, body)
            for i in range(MU):
                gelu(SEQS - 1, i)

        @block.vector
        def _(dve):
            done = 0

            def step(ins):
                nonlocal done
                done += 1
                ins.then_inc(s_setup, 1)

            def layernorm(which, n, src):
                for t in range(TILES):
                    last = nc.vector.bn_stats(ln_stats[:, t, :], src[:, t, :])
                last.then_inc(s_stats[which], 1)
                dve.wait_ge(s_gain, 1)
                dve.wait_ge(s_stats[which], n + 1)
                for t in range(TILES):
                    last = nc.vector.bn_aggr(ln_mv[:, t, :], ln_stats[:, t, :])
                last.then_inc(s_aggr[which], 1)
                dve.wait_ge(s_aggr[which], n + 1)
                nc.vector.tensor_scalar_add(ln_var[:, :], ln_mv[:, :, 1], EPS).then_inc(s_var[which], 1)

            def normalise(which, n, src):
                dve.wait_ge(s_rstd[which], n + 1)
                for t in range(TILES):
                    args = (ln_mv[:, t, 0:1], ln_rstd[:, t:t + 1], ALU.subtract, ALU.mult)
                    nc.vector.tensor_scalar(z[:, t, 0:H], src[:, t, :], *args)
                    last = nc.vector.tensor_scalar(
                        z[:, t, H:ZW].rearrange("p (r n) -> p r n", r=2),
                        src[:, t, 2 * P:H].rearrange("p (o n) -> p o n", o=1).broadcast_to((P, 2, TAIL)), *args)
                last.then_inc(s_z[which], 1)

            def split_x(which, n, j):
                xv, hi, lo, tail = (xv_qkv, xv_mlp)[which], xs_hi[which], xs_lo[which], xs_tail[which]
                dve.wait_ge(s_xv[which], 3 * n + j + 1)
                if j < 2:
                    nc.vector.tensor_copy(hi[:, j, :], xv[:, j, :]).then_inc(s_round[which], 1)
                    dve.wait_ge(s_round[which], 3 * n + j + 1)
                    nc.vector.tensor_tensor(lo[:, j, :], xv[:, j, :], hi[:, j, :], ALU.subtract).then_inc(s_xs[which], 1)
                else:
                    nc.vector.tensor_copy(tail[0:TAIL3, :], xv[0:TAIL3, 2, :]).then_inc(s_round[which], 1)
                    dve.wait_ge(s_round[which], 3 * n + 3)
                    low = slice(TAIL, 2 * TAIL)
                    nc.vector.tensor_tensor(tail[low, :], xv[low, 2, :], tail[low, :], ALU.subtract).then_inc(s_xs[which], 1)

            def heads(ap):
                return ap.rearrange("p (h d) -> p h d", d=HD)

            def qk_chain(q, t):
                n = q * TILES + t
                dve.wait_ge(s_sq, n + 1)
                nc.vector.tensor_reduce(qk_sum[:, :], heads(squares[:, t, :]), AX.X, ALU.add).then_inc(s_qsum, 1)
                dve.wait_ge(s_qsum, n + 1)
                nc.vector.tensor_scalar(qk_var[:, :], qk_sum[:, :], 1.0 / HD, EPS, ALU.mult, ALU.add).then_inc(s_qvar, 1)
                dve.wait_ge(s_qrstd, n + 1)
                for c in (1, 0):
                    last = nc.vector.tensor_tensor(
                        heads(qk_norm[:, t, c * H:(c + 1) * H]), heads(psum[:, 3 * t + c, 0:H]),
                        qk_rstd[:, c * NH:(c + 1) * NH].rearrange("p (h o) -> p h o", o=1).broadcast_to((P, NH, HD)), ALU.mult)
                last.then_inc(s_qkn, 1)
                dve.wait_ge(s_qkn, n + 1)
                dve.wait_ge(s_stk, 4 * q)
                for c in (1, 0):
                    if c == 0:
                        dve.wait_ge(s_qg, n + 1)
                    src = heads(qk_norm[:, t, H:QK] if c else q_gained[:, t, :])
                    step_to, low_at = (HD, 2 * HD) if c else (2 * HD, HD)
                    for r in range(2):
                        last = nc.vector.tensor_copy(qk_stack[:, t, c, :, r * step_to:r * step_to + HD], src)
                    last.then_inc(s_qround, 1)
                    dve.wait_ge(s_qround, 2 * n + 2 - c)
                    last = nc.vector.tensor_tensor(qk_stack[:, t, c, :, low_at:low_at + HD], src,
                                                   qk_stack[:, t, c, :, 0:HD], ALU.subtract)
                last.then_inc(s_stack, 1)

            def k_read(q, t):
                for i in range(2):
                    dve.wait_ge(s_stk, 4 * q + 2 * t + i + 1)
                    dve.wait_ge(s_score, UNITS * q)
                    nc.vector.tensor_copy(kT[:, 4 * i:4 * i + 4, t * P:(t + 1) * P],
                                          psum[:, 7, :].rearrange("p (u n) -> p u n", u=4)).then_inc(s_kT, 1)

            def attn_read(p, g):
                dve.wait_ge(s_pv, GROUPS * p + g + 1)
                dve.wait_ge(s_oT, p * TILES)
                nc.vector.tensor_copy(attn[:, g, :], psum[:, 4 + g % 2, 0:SEQ]).then_inc(s_attn, 1)

            def o_normalise(p, t):
                n = p * TILES + t
                of_head = psum[:, 6 + t, :].rearrange("p (h d) -> p h d", d=VW)
                dve.wait_ge(s_oT, n + 1)
                nc.vector.reciprocal(o_recip[:, :], of_head[:, :, HD]).then_inc(s_recip, 1)
                dve.wait_ge(s_recip, n + 1)
                nc.vector.tensor_tensor(heads(o_norm[:, t, :]), of_head[:, :, 0:HD],
                                        o_recip[:, :].rearrange("p (h o) -> p h o", o=1).broadcast_to((P, NH, HD)),
                                        ALU.mult).then_inc(s_on, 1)

            def o_split_tile(p, t):
                n = p * TILES + t
                dve.wait_ge(s_on, n + 1)
                dve.wait_ge(s_oback, p * TILES)
                nc.vector.tensor_copy(o_split[:, t, 0:H], o_norm[:, t, :])
                nc.vector.tensor_copy(o_split[:, t, H + TAIL:ZW], o_norm[:, t, 2 * P:H]).then_inc(s_oround, 1)
                dve.wait_ge(s_oround, n + 1)
                nc.vector.tensor_tensor(o_split[:, t, ZW:OW], o_norm[:, t, 0:2 * P], o_split[:, t, 0:2 * P], ALU.subtract)
                nc.vector.tensor_tensor(o_split[:, t, H:H + TAIL], o_norm[:, t, 2 * P:H], o_split[:, t, 2 * P:H],
                                        ALU.subtract).then_inc(s_os, 1)

            def residual(p, t):
                n = p * TILES + t
                dve.wait_ge(s_proj, n + 1)
                dve.wait_ge(s_g1, 16 * (p + 1))
                dve.wait_ge(s_x2c, p)
                nc.vector.tensor_tensor(x2[:, t, :], psum[:, 6 + t, 0:H], gate1[:, 0, :], ALU.mult).then_inc(s_pg, 1)
                dve.wait_ge(s_pg, n + 1)
                dve.wait_ge(s_xres, 16 * (p + 1))
                nc.vector.tensor_tensor(x2[:, t, :], x2[:, t, :], x_res[:, t, :], ALU.add).then_inc(s_x2, 1)

            def split_hidden(m, i):
                n = SEQ * len(range(2 * i, min(2 * i + 2, FT)))
                dve.wait_ge(s_gelu, MU * m + i + 1)
                dve.wait_ge(s_down, MU * m + i - 1 if i >= 2 else MU * m)
                nc.vector.tensor_copy(hid_hi[:, i % 2, 0:n], hidden[:, i % 2, 0:n]).then_inc(s_hround, 1)
                dve.wait_ge(s_hround, MU * m + i + 1)
                nc.vector.tensor_tensor(hid_lo[:, i % 2, 0:n], hidden[:, i % 2, 0:n], hid_hi[:, i % 2, 0:n],
                                        ALU.subtract).then_inc(s_hs, 1)

            def output(m):
                dve.wait_ge(s_down, MU * m + MU)
                dve.wait_ge(s_g2, 16 * (m + 1))
                dve.wait_ge(s_x2c, m + 1)
                dve.wait_ge(s_out, 16 * m)
                for t in range(TILES):
                    nc.vector.tensor_tensor(y[:, t, :], psum[:, t, 0:H], gate2[:, :], ALU.mult).then_inc(s_yg, 1)
                    dve.wait_ge(s_yg, m * TILES + t + 1)
                    nc.vector.tensor_tensor(y[:, t, :], y[:, t, :], x2_prev[:, t, :], ALU.add).then_inc(s_y, 1)

            for t in range(TILES):
                nc.vector.memset(qk_stack[:, t, :, :, :].bitcast(F32), 0.0)
            nc.vector.memset(v_ext[:, :, :, :], 0.0)
            nc.vector.memset(mod_all[:, :, :, :], 0.0)
            nc.vector.memset(b2_rows[:, :].bitcast(F32), 0.0)
            nc.vector.memset(ones_r[:, :].bitcast(F32), 1.0)
            for tail in (*xs_tail, o_tail):
                nc.vector.memset(tail[TAIL3:STACK, :].bitcast(F32), 1.0)
            step(nc.vector.memset(silu[KM:KM + 1, :, :], 1.0))
            dve.wait_ge(s_setup, done)
            nc.vector.memset(qk_stack[:, :, 1, :, SHIFT:SROWS].bitcast(F32), 1.0)
            nc.vector.memset(v_ext[:, :, :, HD:HD + 1], 1.0)
            dve.wait_ge(s_ident, 1)
            nc.vector.tensor_copy(ident_r[:, :], ident[:, :]).then_inc(s_const, 1)
            dve.wait_ge(s_tanh, 1)
            step(nc.vector.tensor_scalar(cond_tanh[:, :, :], cond_tanh[:, :, :], 0.5, 0.5, ALU.mult, ALU.add))
            dve.wait_ge(s_setup, done)
            nc.vector.tensor_tensor(silu[0:KM, :, :], cond_tanh[:, :, :], cond[:, :, :], ALU.mult).then_inc(s_silu, 1)
            dve.wait_ge(s_g, 32)
            step(nc.vector.tensor_tensor(gain[:, :], g_both[:, 0, :], g_both[:, 1, :], ALU.mult))
            dve.wait_ge(s_setup, done)
            step(nc.vector.tensor_scalar(gain[:, :], gain[:, :], HD ** -0.5, None, ALU.mult))
            dve.wait_ge(s_setup, done)
            nc.vector.tensor_reduce(bound[:, :], gain[:, :], AX.X, ALU.max, apply_absolute_value=True).then_inc(s_gain, 1)
            dve.wait_ge(s_gain, 1)
            nc.vector.tensor_scalar(flag[:, :], bound[:, :], float(HD), SCORE_BOUND, ALU.mult, ALU.is_gt).then_inc(s_flag, 1)
            dve.wait_ge(s_x, 16)
            layernorm(0, 0, x_ln)
            normalise(0, 0, x_ln)
            dve.wait_ge(s_modmm, 1)
            cols = psum[:, 7, 0:12 * SEQS].rearrange("p (w k j b) -> p w k j b", w=2, k=2, j=3)
            for rows, j in ((P, 0), (P, 1), (TAIL3, 2)):
                for w in range(2):
                    nc.vector.tensor_copy(mod_all[0:rows, 2 * w, j, :], cols[0:rows, w, 0, j, :])
                    last = nc.vector.tensor_scalar_add(mod_all[0:rows, 2 * w + 1, j, :], cols[0:rows, w, 1, j, :], 1.0)
            last.then_inc(s_mod, 1)
            dve.wait_ge(s_gatemm, 1)
            nc.vector.tensor_copy(gate_rows[:, :, :], psum[0:SEQS, 4:6, 0:H]).then_inc(s_gate, 1)
            dve.wait_ge(s_qkvraw, 96)
            rows_of = (P, P, STACK)
            for k, rows in enumerate(rows_of):
                nc.vector.tensor_reduce(col_mean[0:rows, k, :], heads(raw_w[0:rows, k, 0:QK]), AX.X, ALU.add)
            step(nc.vector.memset(bound[:, :], 0.0))
            dve.wait_ge(s_setup, done)
            for k, rows in enumerate(rows_of):
                last = nc.vector.tensor_scalar(col_mean[0:rows, k, :], col_mean[0:rows, k, :], 1.0 / HD, None, ALU.mult)
            step(last)
            dve.wait_ge(s_setup, done)
            for k, rows in enumerate(rows_of):
                last = nc.vector.tensor_tensor(
                    heads(raw_w[0:rows, k, 0:QK]), heads(raw_w[0:rows, k, 0:QK]),
                    col_mean[0:rows, k, :].rearrange("p (h o) -> p h o", o=1).broadcast_to((rows, 2 * NH, HD)), ALU.subtract)
            step(last)
            dve.wait_ge(s_setup, done)
            nc.vector.tensor_copy(w_tail[:, 0:3 * H], raw_w[0:STACK, 2, 0:3 * H])
            step(nc.vector.tensor_copy(w_hi[:, :, 0:3 * H], raw_w[:, 0:2, 0:3 * H]))
            dve.wait_ge(s_setup, done)
            low = slice(2 * TAIL, STACK)
            step(nc.vector.tensor_tensor(w_tail[low, 0:3 * H], raw_w[low, 2, 0:3 * H], w_tail[low, 0:3 * H], ALU.subtract))
            nc.vector.tensor_tensor(w_lo[:, :, 0:3 * H], raw_w[:, 0:2, 0:3 * H], w_hi[:, :, 0:3 * H], ALU.subtract)
            dve.wait_ge(s_setup, done)
            nc.vector.tensor_copy(w_tail[TAIL3:TAIL3 + 1, 0:3 * H], raw_w[TAIL3:TAIL3 + 1, 2, 0:3 * H]).then_inc(s_wqkv, 1)
            for j in range(3):
                split_x(0, 0, j)
            for t in range(TILES):
                qk_chain(0, t)
            k_read(0, 0)
            k_read(0, 1)
            dve.wait_ge(s_wrest, 3)
            needs_shift = dve.value_load(flag[0:1, 0:1], min_val=0, max_val=1)

            def body(p, more, prev):
                with dve.If(needs_shift > 0):
                    for n in range(TILES * GROUPS):
                        t, g = n // GROUPS, n % GROUPS
                        dve.wait_ge(s_ms, TILES * GROUPS * p + n + 1)
                        two = 2 * (n % 2)
                        nc.vector.tensor_reduce(
                            neg_max[:, t, :].rearrange("p (j u) -> p j u", j=2)[:, :, 2 * g:2 * g + 2],
                            psum[:, two:two + 2, :].rearrange("p j (u n) -> p j u n", u=2),
                            AX.X, ALU.max, negate=True).then_inc(s_mx, 1)
                    dve.wait_ge(s_mT, p + 1)
                    dve.wait_ge(s_md, 32 * p)
                    nc.vector.tensor_copy(shiftT[:, :], psum[0:NH, 4, 0:SEQ]).then_inc(s_mc, 1)
                if more:
                    dve.wait_ge(s_x, 16 * (p + 2))
                    layernorm(0, p + 1, x_ln)
                    dve.wait_ge(s_zT[1], 3 * p)
                    normalise(0, p + 1, x_ln)
                attn_read(p, 0)
                attn_read(p, 1)
                if more:
                    dve.wait_ge(s_qkv, (p + 1) * TILES)
                    split_x(0, p + 1, 0)
                    split_x(0, p + 1, 1)
                attn_read(p, 2)
                attn_read(p, 3)
                if more:
                    split_x(0, p + 1, 2)
                for t in range(TILES):
                    o_normalise(p, t)
                    o_split_tile(p, t)
                if more:
                    qk_chain(p + 1, 0)
                if prev:
                    split_hidden(p - 1, 0)
                if more:
                    qk_chain(p + 1, 1)
                if prev:
                    split_hidden(p - 1, 1)
                residual(p, 0)
                if prev:
                    split_hidden(p - 1, 2)
                residual(p, 1)
                dve.wait_ge(s_x2, p * TILES + TILES)
                layernorm(1, p, x2)
                if prev:
                    split_hidden(p - 1, 3)
                if more:
                    dve.wait_ge(s_zT[0], 3 * (p + 2))
                else:
                    dve.wait_ge(s_zT[0], 3 * (p + 1))
                normalise(1, p, x2)
                if prev:
                    split_hidden(p - 1, 4)
                    output(p - 1)
                dve.wait_ge(s_x2, p * TILES + TILES)
                dve.wait_ge(s_y, p * TILES)
                nc.vector.tensor_copy(x2_prev, x2).then_inc(s_x2c, 1)
                if more:
                    k_read(p + 1, 0)
                    k_read(p + 1, 1)
                if prev:
                    dve.wait_ge(s_up, MU * p)
                for j in range(3):
                    split_x(1, p, j)

            passes(dve, body)
            for i in range(MU):
                split_hidden(SEQS - 1, i)
            output(SEQS - 1)


def kernel(x, cond_1152, L0_cond_w_mod, L0_cond_b_mod, L0_cond_w_qkv, L0_cond_b_qkv, L0_cond_g_q, L0_cond_g_k,
           L0_cond_w_proj, L0_cond_b_proj, L0_cond_w1, L0_cond_b1, L0_cond_w2, L0_cond_b2):
    import numpy as np
    from concourse import bacc
    from concourse.bass_utils import run_bass_kernel_spmd

    arrays = {"x": x, "condT": np.asarray(cond_1152).T, "w_mod": L0_cond_w_mod, "b_mod": L0_cond_b_mod,
              "w_qkv": L0_cond_w_qkv, "b_qkv": L0_cond_b_qkv, "g_q": L0_cond_g_q, "g_k": L0_cond_g_k,
              "w_proj": L0_cond_w_proj, "b_proj": L0_cond_b_proj, "w1": L0_cond_w1, "b1": L0_cond_b1,
              "w2": L0_cond_w2, "b2": L0_cond_b2}
    nc = bacc.Bacc("TRN2", target_bir_lowering=False, num_devices=1)
    feeds, args = {}, []
    for name, a in arrays.items():
        a = np.ascontiguousarray(a)
        feeds[f"in_{name}"] = a
        args.append(nc.dram_tensor(f"in_{name}", a.shape, mybir.dt.from_np(a.dtype), kind="ExternalInput").ap())
    args.append(nc.dram_tensor("gate_scratch", (SEQS, 2 * H), F32, kind="Internal").ap())
    args.append(nc.dram_tensor("out_0", x.shape, F32, kind="ExternalOutput").ap())
    dit_block(nc, *args)
    r = run_bass_kernel_spmd(nc, [feeds], core_ids=[0])
    return r.results[0]["out_0"]
```

```python
from contextlib import ExitStack

import concourse.bass as bass
from concourse import mybir

F32 = mybir.dt.float32
F32R = mybir.dt.float32r
I32 = mybir.dt.int32
ACT = mybir.ActivationFunctionType
ALU = mybir.AluOpType
AX = mybir.AxisListType

P = 128
SEQS, SEQ, H = 8, 256, 288
NH = 16
HD = H // NH
MLP = 4 * H
TILES = SEQ // P
UNITS = NH // 2
GROUPS = NH // 4
FT = MLP // P
MU = (FT + 1) // 2
TAIL = H - 2 * P
TAIL3 = 3 * TAIL
STACK = TAIL3 + 2
ZW = 2 * P + TAIL3
OW = ZW + 2 * P
KM = H // 3
HALF = 64
SHIFT = 3 * HD
SROWS = SHIFT + 1
VW = 32
NMOD = 6 * H
EPS = 1e-6
SCORE_BOUND = 60.0
RSQRT_MAGIC = float(0x5F3759DF)
RSQRT_STEPS_V = 10
RSQRT_STEPS = 12
W_QKV, W_PROJ, W_1 = 0, 3 * H, 4 * H
W_ALL = 4 * H + MLP
QK = 2 * H


def dit_block(nc, x, condT, w_mod, b_mod, w_qkv, b_qkv, g_q, g_k, w_proj, b_proj, w1, b1, w2, b2,
              gate_scratch, out):
    x_seqs = x.rearrange("s (t p) f -> s p t f", p=P)
    out_seqs = out.rearrange("s (t p) f -> s p t f", p=P)

    with ExitStack() as ctx:
        def sb(name, shape, dt=F32):
            return ctx.enter_context(nc.sbuf_tensor(name, shape, dt))

        def sem(name):
            return ctx.enter_context(nc.semaphore(name))

        w_hi = sb("w_hi", [P, 2, W_ALL], F32R)
        w_lo = sb("w_lo", [P, 2, W_ALL], F32R)
        w_tail = sb("w_tail", [STACK, W_ALL], F32R)
        w2_hi = sb("w2_hi", [P, FT, H], F32R)
        w2_lo = sb("w2_lo", [P, FT, H], F32R)
        b2_rows = sb("b2_rows", [P, H], F32R)
        arena = sb("arena", [P, 3 * W_ALL + 3 * NMOD + FT * H])
        raw_w = arena[:, 0:3 * W_ALL].rearrange("p (k n) -> p k n", k=3)
        raw_mod = arena[:, 3 * W_ALL:3 * W_ALL + 3 * NMOD].rearrange("p (k n) -> p k n", k=3)
        raw_w2 = arena[:, 3 * W_ALL + 3 * NMOD:].rearrange("p (k n) -> p k n", k=FT)

        def carve(start, *shape):
            size = shape[0] * shape[1]
            return arena[:, start:start + size].rearrange("p (u n) -> p u n", u=shape[0]), start + size

        at = 0
        prob, at = carve(at, 4, 4 * SEQ)
        o_norm, at = carve(at, TILES, H)
        xv_mlp, at = carve(at, 3, SEQ)
        attn, at = carve(at, GROUPS, SEQ)
        assert at <= 3 * W_ALL
        at = 3 * W_ALL
        squares, at = carve(at, 2, QK)
        qk_norm, at = carve(at, 2, QK)
        q_gained, at = carve(at, 2, H)
        hidden, at = carve(at, 2, 2 * SEQ)
        assert at <= 3 * W_ALL + 3 * NMOD
        at = 3 * W_ALL + 3 * NMOD
        y, at = carve(at, TILES, H)
        x2_prev, at = carve(at, TILES, H)
        x2, at = carve(at, TILES, H)
        x_res, at = carve(at, TILES, H)
        gate1, at = carve(at, 1, H)
        assert at <= 3 * W_ALL + 3 * NMOD + FT * H
        x_ln = sb("x_ln", [P, TILES, H])
        z = sb("z", [P, TILES, ZW])
        xv_qkv = sb("xv_qkv", [P, 3, SEQ])
        gate2 = sb("gate2", [P, H])
        xs_hi = [sb(f"xs_hi_{n}", [P, 2, SEQ], F32R) for n in ("qkv", "mlp")]
        xs_lo = [sb(f"xs_lo_{n}", [P, 2, SEQ], F32R) for n in ("qkv", "mlp")]
        xs_tail = [sb(f"xs_tail_{n}", [STACK, SEQ], F32R) for n in ("qkv", "mlp")]
        o_split = sb("o_split", [P, TILES, OW], F32R)
        o_stack = sb("o_stack", [P, TILES, 4 * P], F32R)
        o_tail = sb("o_tail", [STACK, SEQ], F32R)
        qk_stack = sb("qk_stack", [P, TILES, 2, NH, HALF], F32R)
        qT = sb("qT", [P, UNITS, SEQ], F32R)
        kT = sb("kT", [P, UNITS, SEQ], F32R)
        v_ext = sb("v_ext", [P, TILES, NH, VW])
        hid_hi = sb("hid_hi", [P, 2, 2 * SEQ], F32R)
        hid_lo = sb("hid_lo", [P, 2, 2 * SEQ], F32R)
        ident = sb("ident", [P, P])
        ident_r = sb("ident_r", [P, P], F32R)
        ones_r = sb("ones_r", [P, P], F32R)
        cond = sb("cond", [KM, 3, SEQS])
        cond_tanh = sb("cond_tanh", [KM, 3, SEQS])
        silu = sb("silu", [KM + 1, 3, SEQS])
        mod_all = sb("mod_all", [P, 4, 3, SEQS])
        mod_cur = [sb(f"mod_cur_{n}", [P, 2, 3]) for n in ("qkv", "mlp")]
        gate_rows = sb("gate_rows", [SEQS, 2, H])
        col_mean = sb("col_mean", [P, 3, 2 * NH])
        g_both = sb("g_both", [P, 2, HD])
        gain = sb("gain", [P, HD])
        bound = sb("bound", [P, 1])
        flag = sb("flag", [P, 1], I32)
        minus_half = sb("minus_half", [P, 2 * NH])
        three_halves = sb("three_halves", [P, 2 * NH])
        table_in = sb("table_in", [P, 1])
        table_out = sb("table_out", [P, 1])
        ln_stats = sb("ln_stats", [P, TILES, 6])
        ln_mv = sb("ln_mv", [P, TILES, 2])
        ln_var = sb("ln_var", [P, TILES])
        ln_rstd = sb("ln_rstd", [P, TILES])
        qk_sum = sb("qk_sum", [P, 2 * NH])
        qk_var = sb("qk_var", [P, TILES, 2 * NH])
        half_v, qk_half = sb("half_v", [P, 2 * NH]), sb("qk_half", [P, 2 * NH])
        square_v, qk_square = sb("square_v", [P, 2 * NH]), sb("qk_square", [P, 2 * NH])
        qk_rstd = sb("qk_rstd", [P, TILES, 2 * NH])
        o_recip = sb("o_recip", [P, NH])
        neg_max = sb("neg_max", [P, TILES, NH])
        shiftT = sb("shiftT", [NH, SEQ])

        psum = ctx.enter_context(nc.psum_tensor("psum", [P, 8, 512], F32))
        hidden_bank = (2, 5)

        def score_bank(u):
            return 4 if u == 1 else 2 if u % 2 == 0 else 0

        ln_bank = ((6, 7, 6), (4, 5, 3))

        s_const = sem("constants_made")
        s_ident0, s_ident = sem("identity_zeroed"), sem("identity_ready")
        s_cond, s_g = sem("cond_loaded"), sem("gains_loaded")
        s_modraw, s_qkvraw, s_projraw, s_w1raw, s_w2raw = (sem(f"{n}_loaded") for n in ("w_mod", "w_qkv", "w_proj", "w1", "w2"))
        s_setup, s_bias0 = sem("vector_setup_step"), sem("bias_rows_zeroed")
        s_centred, s_low = sem("w_qkv_centred"), sem("full_tiles_low_halves")
        s_qkvhi, s_projhi, s_w1hi, s_w2hi = (sem(f"{n}_rounded") for n in ("w_qkv", "w_proj", "w1", "w2"))
        s_wqkv, s_wproj, s_w1, s_w2 = (sem(f"{n}_split") for n in ("w_qkv", "w_proj", "w1", "w2"))
        s_tanh, s_silu = sem("tanh_done"), sem("silu_ready")
        s_modmm, s_gatemm = sem("mod_products_done"), sem("gate_products_done")
        s_mod, s_gate, s_stored = sem("mod_columns_ready"), sem("gate_rows_ready"), sem("gate_rows_stored")
        s_gain, s_flag = sem("gain_ready"), sem("flag_ready")
        s_x, s_xres, s_g1, s_g2 = sem("x_loaded"), sem("x_res_loaded"), sem("gate1_loaded"), sem("gate2_loaded")
        both = ("qkv", "mlp")
        s_stats = [sem(f"ln_stats_{n}") for n in both]
        s_aggr = [sem(f"ln_aggregated_{n}") for n in both]
        s_var = [sem(f"ln_variance_{n}") for n in both]
        s_rstd = [sem(f"ln_rstd_{n}") for n in both]
        s_z = [sem(f"z_ready_{n}") for n in both]
        s_modc = [sem(f"mod_copied_{n}") for n in both]
        s_zT = [sem(f"z_transposed_{n}") for n in both]
        s_xv = [sem(f"x_modulated_{n}") for n in both]
        s_x2round = sem("x_rounded_mlp")
        s_xs = [sem(f"x_split_{n}") for n in both]
        s_qkv = sem("qkv_done")
        s_sq, s_v = sem("squares_done"), sem("v_read")
        s_qsum, s_qvar, s_qrstd = sem("square_sums_done"), sem("qk_variance"), sem("qk_rstd_ready")
        s_newton_v, s_newton = sem("vector_newton_step"), sem("pool_newton_step")
        s_qkn, s_qg = sem("qk_normalised"), sem("q_gained_ready")
        s_qround, s_stack = sem("qk_rounded"), sem("qk_stack_ready")
        s_st, s_stq, s_stk = sem("stack_tile_done"), sem("q_stack_transposed"), sem("k_stack_transposed")
        s_qT, s_qlast, s_kT = sem("qT_written"), sem("last_qT_written"), sem("kT_written")
        s_score, s_exp = sem("scores_done"), sem("exp_done")
        s_pv, s_attn = sem("attn_group_done"), sem("attn_group_read")
        s_oT, s_recip, s_on = sem("attn_transposed"), sem("row_sums_inverted"), sem("o_normalised")
        s_oround, s_os = sem("o_rounded"), sem("o_split_ready")
        s_oback, s_ostack = sem("o_transposed"), sem("o_stack_written")
        s_proj, s_pg, s_x2 = sem("proj_done"), sem("proj_gated"), sem("x2_ready")
        s_x2c = sem("x2_handed_on")
        s_up, s_gelu = sem("mlp_up_done"), sem("gelu_done")
        s_hs, s_down = sem("hidden_split"), sem("mlp_down_done")
        s_yg, s_y, s_out = sem("mlp_gated"), sem("y_ready"), sem("y_stored")
        s_ms, s_mx = sem("shift_scores_done"), sem("shift_maxima_done")
        s_mT, s_mc, s_md = sem("maxima_transposed"), sem("maxima_copied"), sem("shift_rows_written")

        block = ctx.enter_context(nc.Block())

        def passes(engine, body):
            body(0, True, False, False)
            body(1, True, True, False)
            with engine.Fori(2, SEQS - 1) as p:
                body(p, True, True, True)
            body(SEQS - 1, False, True, True)

        def dense(pe, dst, hi, lo, tail, cols, act_moves):
            terms = [(hi(0), w_hi[:, 0, cols]), (hi(1), w_hi[:, 1, cols]),
                     (hi(0), w_lo[:, 0, cols]), (hi(1), w_lo[:, 1, cols]),
                     (lo(0), w_hi[:, 0, cols]), (lo(1), w_hi[:, 1, cols]),
                     (tail, w_tail[:, cols])]
            for n, (a, w) in enumerate(terms):
                lhsT, rhs = (w, a) if act_moves else (a, w)
                last = nc.tensor.matmul(dst, lhsT, rhs, start=(n == 0), stop=(n == len(terms) - 1))
            return last

        @block.sync
        def _(sp):
            def row(v):
                return v.rearrange("(o n) -> o n", o=1)

            sp.dma_start(cond[:, :, :], condT.rearrange("(k p) b -> p k b", p=KM)).then_inc(s_cond, 16)
            for i, g in enumerate((g_q, g_k)):
                sp.dma_start(g_both[:, i, :], row(g).broadcast_to((P, HD))).then_inc(s_g, 16)
            sp.dma_start(x_ln[:, :, :], x_seqs[0]).then_inc(s_x, 16)
            sp.dma_start(raw_mod[0:KM, :, :], w_mod.rearrange("(k p) n -> p k n", p=KM)).then_inc(s_modraw, 16)
            sp.dma_start(raw_mod[KM:KM + 1, 2, :], row(b_mod)).then_inc(s_modraw, 16)
            for w, b, c, s in ((w_qkv, b_qkv, W_QKV, s_qkvraw), (w_proj, b_proj, W_PROJ, s_projraw), (w1, b1, W_1, s_w1raw)):
                n = w.shape[1]
                sp.dma_start(raw_w[:, 0:2, c:c + n], w[0:2 * P, :].rearrange("(k p) n -> p k n", p=P)).then_inc(s, 16)
                for r in range(3):
                    sp.dma_start(raw_w[r * TAIL:(r + 1) * TAIL, 2, c:c + n], w[2 * P:H, :]).then_inc(s, 16)
                for r in range(2):
                    sp.dma_start(raw_w[TAIL3 + r:TAIL3 + r + 1, 2, c:c + n], row(b)).then_inc(s, 16)
            sp.dma_start(raw_w2, w2.rearrange("(k p) n -> p k n", p=P)).then_inc(s_w2raw, 16)
            for r in range(2):
                sp.dma_start(gate2[r:r + 1, :], row(b2)).then_inc(s_w2raw, 16)
            sp.wait_ge(s_gate, 1)
            sp.dma_start(gate_scratch, gate_rows[:, :, :].rearrange("b g f -> b (g f)")).then_inc(s_stored, 16)
            sp.wait_ge(s_stored, 16)
            sp.wait_ge(s_flag, 1)
            needs_shift = sp.value_load(flag[0:1, 0:1], min_val=0, max_val=1)
            for s in (s_wproj, s_w1, s_w2):
                sp.wait_ge(s, 1)

            def body(p, more, prev, older):
                with sp.If(needs_shift > 0):
                    sp.wait_ge(s_mc, p + 1)
                    for j in range(2):
                        at_row = HALF * j + SHIFT
                        sp.dma_start(qT[at_row:at_row + 1, :, :].bitcast(F32),
                                     shiftT[UNITS * j:UNITS * (j + 1), :]).then_inc(s_md, 16)
                if more:
                    sp.wait_ge(s_z[0], p + 1)
                    sp.dma_start(x_ln[:, :, :], x_seqs[p + 1]).then_inc(s_x, 16)
                if older:
                    store(p - 2)
                sp.wait_ge(s_x2, p * TILES)
                sp.dma_start(x_res[:, :, :], x_seqs[p]).then_inc(s_xres, 16)
                sp.wait_ge(s_pg, p * TILES)
                sp.dma_start(gate1[:, 0, :], gate_scratch[bass.ds(p, 1), 0:H].broadcast_to((P, H))).then_inc(s_g1, 16)
                if prev:
                    load_gate2(p - 1)

            def load_gate2(m):
                sp.wait_ge(s_yg, m * TILES)
                sp.dma_start(gate2[:, :], gate_scratch[bass.ds(m, 1), H:2 * H].broadcast_to((P, H))).then_inc(s_g2, 16)

            def store(m):
                sp.wait_ge(s_y, m * TILES + TILES)
                sp.dma_start(out_seqs[m], y[:, :, :]).then_inc(s_out, 16)

            passes(sp, body)
            store(SEQS - 2)
            load_gate2(SEQS - 1)
            store(SEQS - 1)
            sp.wait_ge(s_out, 16 * SEQS)

        @block.gpsimd
        def _(pool):
            nc.gpsimd.memset(ident[:, :], 0.0).then_inc(s_ident0, 1)
            nc.gpsimd.memset(three_halves[:, :], 1.5)
            nc.gpsimd.memset(minus_half[:, :], -0.5).then_inc(s_const, 1)
            pool.wait_ge(s_ident0, 1)
            nc.gpsimd.affine_select(out=ident[:, :], in_=ident[:, :], compare_op=ALU.not_equal, fill=1.0, base=0,
                                    pattern=[[-1, P]], channel_multiplier=1).then_inc(s_ident, 1)

            def power(s_in, s_result, dst, src, n):
                pool.wait_ge(s_in, n)
                nc.gpsimd.tensor_tensor(dst, src, minus_half[:, 0:src.shape[1]], ALU.pow).then_inc(s_result, 1)

            def ln_power(which, n):
                power(s_var[which], s_rstd[which], ln_rstd[:, :], ln_var[:, :], n + 1)

            def copy_mod(which, n):
                pool.wait_ge(s_mod, 1)
                pool.wait_ge(s_xv[which], 3 * n)
                nc.gpsimd.tensor_copy(mod_cur[which][:, :, :], mod_all[:, 2 * which:2 * which + 2, :, n]).then_inc(s_modc[which], 1)

            def qk_rsqrt(q):
                steps = q * RSQRT_STEPS
                var, r = qk_var[:, 1, :], qk_rstd[:, 1, :]
                pool.wait_ge(s_qvar, q * TILES + 2)
                pool.wait_ge(s_qkn, q * TILES)
                nc.gpsimd.tensor_tensor(qk_half[:, :], var, minus_half[:, :], ALU.mult)
                nc.gpsimd.tensor_scalar(r.bitcast(I32), var.bitcast(I32), -0.5, RSQRT_MAGIC, ALU.mult, ALU.add).then_inc(s_newton, 1)
                for i in range(3):
                    pool.wait_ge(s_newton, steps + 4 * i + 1)
                    nc.gpsimd.tensor_tensor(qk_square[:, :], r, r, ALU.mult).then_inc(s_newton, 1)
                    pool.wait_ge(s_newton, steps + 4 * i + 2)
                    nc.gpsimd.tensor_tensor(qk_square[:, :], qk_square[:, :], qk_half[:, :], ALU.mult).then_inc(s_newton, 1)
                    pool.wait_ge(s_newton, steps + 4 * i + 3)
                    nc.gpsimd.tensor_tensor(qk_square[:, :], qk_square[:, :], three_halves[:, :], ALU.add).then_inc(s_newton, 1)
                    pool.wait_ge(s_newton, steps + 4 * i + 4)
                    last = nc.gpsimd.tensor_tensor(r, r, qk_square[:, :], ALU.mult)
                    if i < 2:
                        last.then_inc(s_newton, 1)
                last.then_inc(s_qrstd, 1)

            def qk_gain(q, t):
                n = q * TILES + t
                pool.wait_ge(s_qkn, n + 1)
                nc.gpsimd.tensor_tensor(
                    q_gained[:, t, :].rearrange("p (h d) -> p h d", d=HD),
                    qk_norm[:, t, 0:H].rearrange("p (h d) -> p h d", d=HD),
                    gain[:, :].rearrange("p (o d) -> p o d", o=1).broadcast_to((P, NH, HD)), ALU.mult).then_inc(s_qg, 1)

            def split_low(i, c, n, s_hi, s_split):
                cols, low = slice(c, c + n), slice(2 * TAIL, STACK)
                pool.wait_ge(s_hi, 1)
                nc.gpsimd.tensor_tensor(w_lo[:, :, cols], raw_w[:, 0:2, cols], w_hi[:, :, cols], ALU.subtract).then_inc(s_low, 1)
                pool.wait_ge(s_low, i + 1)
                nc.gpsimd.tensor_tensor(w_tail[low, cols], raw_w[low, 2, cols], w_tail[low, cols], ALU.subtract).then_inc(s_split, 1)

            pool.wait_ge(s_const, 2)
            ln_power(0, 0)
            split_low(0, W_PROJ, H, s_projhi, s_wproj)
            pool.wait_ge(s_wproj, 1)
            split_low(1, W_1, MLP, s_w1hi, s_w1)
            pool.wait_ge(s_w1, 1)
            pool.wait_ge(s_gain, 1)
            for t in range(TILES):
                if t == 1:
                    qk_rsqrt(0)
                qk_gain(0, t)

            def body(p, more, prev, older):
                if more:
                    ln_power(0, p + 1)
                    copy_mod(0, p + 1)
                    qk_gain(p + 1, 0)
                    qk_rsqrt(p + 1)
                    qk_gain(p + 1, 1)
                ln_power(1, p)
                copy_mod(1, p)

            passes(pool, body)

        @block.tensor
        def _(pe):
            pe.wait_ge(s_silu, 1)
            pe.wait_ge(s_modraw, 32)
            def mod_product(dst, lhs, rhs):
                for k in range(3):
                    rows = KM + (k == 2)
                    last = nc.tensor.matmul(dst, lhs(k, rows), rhs(k, rows), start=(k == 0), stop=(k == 2))
                return last

            for i, kind in enumerate((0, 1, 3, 4)):
                for j in range(3):
                    parts = [(0, P, j * P)] if j < 2 else [(r * TAIL, TAIL, 2 * P) for r in range(3)]
                    for row0, m, col0 in parts:
                        at = (3 * i + j) * SEQS
                        last = mod_product(psum[row0:row0 + m, 7, at:at + SEQS],
                                           lambda k, rows: raw_mod[0:rows, k, kind * H + col0:kind * H + col0 + m],
                                           lambda k, rows: silu[0:rows, k, :])
            last.then_inc(s_modmm, 1)
            def ln_transpose(which, n, j):
                pe.wait_ge(s_z[which], n + 1)
                rows = P if j < 2 else TAIL3
                for t in range(TILES):
                    last = nc.tensor.transpose(psum[0:rows, ln_bank[which][j], t * P:(t + 1) * P],
                                               z[:, t, j * P:j * P + rows], ident[:, :])
                last.then_inc(s_zT[which], 1)

            def qkv(q, t, parts=range(3)):
                pe.wait_ge(s_xs[0], 3 * q + 3)
                tok = slice(t * P, (t + 1) * P)
                for c in parts:
                    last = dense(pe, psum[:, 3 * t + c, 0:H], lambda k: xs_hi[0][:, k, tok],
                                 lambda k: xs_lo[0][:, k, tok], xs_tail[0][:, tok],
                                 slice(W_QKV + c * H, W_QKV + (c + 1) * H), False)
                if parts[-1] == 2:
                    last.then_inc(s_qkv, 1)

            def stack_transpose(q, n):
                t, i = n // 2, n % 2
                pe.wait_ge(s_stack, q * TILES + t + 1)
                for c, s_done, read in ((0, s_stq, (s_qT, 3 * q + n)), (1, s_stk, (s_kT, 4 * q + n))):
                    if n > 0:
                        pe.wait_ge(*read)
                    for k in range(4):
                        u = 4 * i + k
                        last = nc.tensor.transpose(
                            psum[:, 6 + c, k * P:(k + 1) * P].bitcast(F32R),
                            qk_stack[:, t, c, 2 * u:2 * u + 2, :].rearrange("p h r -> p (h r)"), ident_r[:, :])
                    last.then_inc(s_done, 1)

            def scores(p, u):
                if u % 4 == 0:
                    pe.wait_ge(s_kT, 4 * p + 3 + u // 4)
                if u == 0:
                    pe.wait_ge(s_qT, 3 * p + 3)
                if u == 4:
                    pe.wait_ge(s_qlast, p + 1)
                if u == 2 or u >= 4:
                    pe.wait_ge(s_exp, UNITS * p + u - 1)
                two = score_bank(u)
                for kt in range(TILES):
                    for j in range(2):
                        rows = slice(HALF * j, HALF * j + SROWS)
                        last = nc.tensor.matmul(psum[:, two + j, kt * SEQ:(kt + 1) * SEQ],
                                                kT[rows, u, kt * P:(kt + 1) * P], qT[rows, u, :],
                                                start=True, stop=True)
                last.then_inc(s_score, 1)

            def values(p, g):
                pe.wait_ge(s_exp, UNITS * p + 2 * g + 2)
                if g >= 2:
                    pe.wait_ge(s_attn, GROUPS * p + g - 1)
                for kt in range(TILES):
                    for c in range(4):
                        u, j = 2 * g + c // 2, c % 2
                        last = nc.tensor.matmul(
                            psum[32 * c:32 * c + 32, 4 + g % 2, 0:SEQ], v_ext[:, kt, 4 * g + c, :],
                            prob[:, u % 4, j * 2 * SEQ + kt * SEQ:j * 2 * SEQ + (kt + 1) * SEQ],
                            start=(kt == 0), stop=(kt == TILES - 1))
                last.then_inc(s_pv, 1)

            def o_back(p, t):
                pe.wait_ge(s_os, p * TILES + t + 1)
                if t == 0:
                    pe.wait_ge(s_on, p * TILES + TILES)
                else:
                    pe.wait_ge(s_ostack, 4 * p + 2 * t)
                for i, c in enumerate((0, P, ZW, ZW + P)):
                    nc.tensor.transpose(psum[:, 6, i * P:(i + 1) * P].bitcast(F32R), o_split[:, t, c:c + P], ident_r[:, :])
                nc.tensor.transpose(psum[0:TAIL3, 7, 0:P].bitcast(F32R), o_split[:, t, 2 * P:ZW],
                                    ident_r[:, :]).then_inc(s_oback, 1)

            def project(p, t):
                pe.wait_ge(s_ostack, 4 * p + 4)
                dense(pe, psum[:, 6 + t, 0:H], lambda k: o_stack[:, t, k * P:(k + 1) * P],
                      lambda k: o_stack[:, t, (2 + k) * P:(3 + k) * P], o_tail[:, t * P:(t + 1) * P],
                      slice(W_PROJ, W_PROJ + H), False).then_inc(s_proj, 1)

            def unit_tiles(i):
                return range(2 * i, min(2 * i + 2, FT))

            def up(m, i):
                if i >= 2:
                    pe.wait_ge(s_gelu, MU * m + i - 1)
                for f in unit_tiles(i):
                    last = dense(pe, psum[:, hidden_bank[i % 2], (f % 2) * SEQ:(f % 2 + 1) * SEQ],
                                 lambda k: xs_hi[1][:, k, :], lambda k: xs_lo[1][:, k, :], xs_tail[1][:, :],
                                 slice(W_1 + f * P, W_1 + (f + 1) * P), True)
                last.then_inc(s_up, 1)

            def down(m, i):
                pe.wait_ge(s_hs, MU * m + i + 1)
                for t in range(TILES):
                    if i == 0:
                        nc.tensor.matmul(psum[:, t, 0:H], ones_r[:, :], b2_rows[:, :], start=True, stop=False)
                    for f in unit_tiles(i):
                        tok = slice((f % 2) * SEQ + t * P, (f % 2) * SEQ + (t + 1) * P)
                        for n, (a, w) in enumerate(((hid_hi, w2_hi), (hid_hi, w2_lo), (hid_lo, w2_hi))):
                            last = nc.tensor.matmul(psum[:, t, 0:H], a[:, i % 2, tok], w[:, f, :],
                                                    start=False, stop=(f == FT - 1 and n == 2))
                last.then_inc(s_down, 1)

            def mlp(m, qk_read, between, behind):
                pe.wait_ge(s_xs[1], 3 * m + 3)
                up(m, 0)
                between()
                up(m, 1)
                if qk_read is not None:
                    pe.wait_ge(s_qkn, qk_read)
                for i in range(MU - 1):
                    down(m, i)
                    if i + 2 < MU:
                        up(m, i + 2)
                    behind(i)

            pe.wait_ge(s_mod, 1)
            pe.wait_ge(s_ident, 1)
            ln_transpose(0, 0, 0)
            ln_transpose(0, 0, 1)
            pe.wait_ge(s_xv[0], 1)
            ln_transpose(0, 0, 2)
            for i, kind in enumerate((2, 5)):
                last = mod_product(psum[0:SEQS, 4 + i, 0:H], lambda k, rows: silu[0:rows, k, :],
                                   lambda k, rows: raw_mod[0:rows, k, kind * H:(kind + 1) * H])
            last.then_inc(s_gatemm, 1)
            pe.wait_ge(s_wqkv, 1)
            qkv(0, 0)
            pe.wait_ge(s_gate, 1)
            qkv(0, 1)
            pe.wait_ge(s_xv[0], 3)
            pe.wait_ge(s_const, 2)
            for n in range(4):
                stack_transpose(0, n)
            pe.wait_ge(s_flag, 1)
            needs_shift = pe.value_load(flag[0:1, 0:1], min_val=0, max_val=1)

            def body(p, more, prev, older):
                pe.wait_ge(s_v, p * TILES + TILES)
                pe.wait_ge(s_qkn, p * TILES + TILES)
                if prev:
                    pe.wait_ge(s_xv[1], 3 * p)
                if older:
                    pe.wait_ge(s_gelu, (p - 1) * MU)

                def finish():
                    if older:
                        down(p - 2, MU - 1)

                with pe.If(needs_shift > 0):
                    finish()
                    if older:
                        pe.wait_ge(s_yg, (p - 1) * TILES)
                    pe.wait_ge(s_qT, 3 * p + 3)
                    pe.wait_ge(s_qlast, p + 1)
                    pe.wait_ge(s_kT, 4 * p + 4)
                    for n in range(TILES * GROUPS):
                        t, g = n // GROUPS, n % GROUPS
                        if n >= 2:
                            pe.wait_ge(s_mx, TILES * GROUPS * p + n - 1)
                        for c in range(4):
                            u, j = 2 * g + c // 2, c % 2
                            rows = slice(HALF * j, HALF * j + SHIFT)
                            last = nc.tensor.matmul(psum[:, 2 * (n % 2) + j, (c // 2) * SEQ:(c // 2 + 1) * SEQ],
                                                    qT[rows, u, t * P:(t + 1) * P], kT[rows, u, :],
                                                    start=True, stop=True)
                        last.then_inc(s_ms, 1)
                    pe.wait_ge(s_mx, TILES * GROUPS * (p + 1))
                    for t in range(TILES):
                        last = nc.tensor.transpose(psum[0:NH, 4, t * P:(t + 1) * P], neg_max[:, t, :], ident[:, :])
                    last.then_inc(s_mT, 1)
                    pe.wait_ge(s_md, 32 * (p + 1))
                    scores(p, 0)
                    scores(p, 1)
                with pe.Else():
                    scores(p, 0)
                    scores(p, 1)
                    finish()
                for g in range(GROUPS):
                    if g < GROUPS - 1:
                        scores(p, 2 * g + 2)
                        if g == 0:
                            values(p, g)
                            if older:
                                pe.wait_ge(s_yg, (p - 1) * TILES)
                        scores(p, 2 * g + 3)
                    if more and g == 1:
                        ln_transpose(0, p + 1, 0)
                        ln_transpose(0, p + 1, 1)
                    if more and g == 2:
                        pe.wait_ge(s_xv[0], 3 * p + 4)
                        ln_transpose(0, p + 1, 2)
                    if g > 0:
                        values(p, g)
                if more:
                    pe.wait_ge(s_xv[0], 3 * p + 6)
                    qkv(p + 1, 0, range(1))
                pe.wait_ge(s_attn, GROUPS * p + GROUPS)
                for t in range(TILES):
                    for g in range(GROUPS):
                        last = nc.tensor.transpose(psum[:, 6 + t, g * P:(g + 1) * P],
                                                   attn[:, g, t * P:(t + 1) * P], ident[:, :])
                    last.then_inc(s_oT, 1)
                if more:
                    qkv(p + 1, 0, range(1, 3))
                    qkv(p + 1, 1, range(1))
                if not prev:
                    pe.wait_ge(s_wproj, 1)
                o_back(p, 0)
                if more:
                    qkv(p + 1, 1, range(1, 2))
                o_back(p, 1)
                if more:
                    qkv(p + 1, 1, range(2, 3))
                if not prev:
                    project(p, 0)
                    project(p, 1)

                def between():
                    project(p, 0)
                    project(p, 1)
                    if more:
                        pe.wait_ge(s_v, (p + 1) * TILES + TILES)

                def behind(i):
                    if more:
                        if i == 0:
                            pe.wait_ge(s_pg, (p + 1) * TILES)
                        stack_transpose(p + 1, i)
                    if i == 2:
                        if more:
                            pe.wait_ge(s_qkn, (p + 1) * TILES + TILES)
                            pe.wait_ge(s_v, (p + 1) * TILES + TILES)
                        if prev:
                            pe.wait_ge(s_gelu, MU * (p - 1) + 4)
                        for j in range(3):
                            ln_transpose(1, p, j)

                if prev:
                    if more:
                        pe.wait_ge(s_v, (p + 1) * TILES + 1)
                    mlp(p - 1, (p + 1) * TILES + 1 if more else None, between, behind)
                else:
                    for i in range(MU - 1):
                        behind(i)
                if not prev:
                    pe.wait_ge(s_w1, 1)
                    pe.wait_ge(s_w2, 1)

            passes(pe, body)
            down(SEQS - 2, MU - 1)
            pe.wait_ge(s_yg, (SEQS - 1) * TILES)
            mlp(SEQS - 1, None, lambda: None, lambda i: None)
            down(SEQS - 1, MU - 1)

        @block.scalar
        def _(act):
            act.wait_ge(s_cond, 16)
            nc.scalar.activation(cond_tanh[:, :, :], cond[:, :, :], ACT.Tanh, scale=0.5).then_inc(s_tanh, 1)

            def modulate(which, n, j):
                xv = (xv_qkv, xv_mlp)[which]
                rows = P if j < 2 else TAIL3
                act.wait_ge(s_zT[which], 3 * n + j + 1)
                act.wait_ge(s_modc[which], n + 1)
                act.wait_ge(s_xs[which], 3 * n)
                dsts = [xv[0:rows, j, :]]
                if which == 0:
                    act.wait_ge(s_qkv, TILES * n)
                    dsts.append(xs_hi[0][:, j, :] if j < 2 else xs_tail[0][0:TAIL3, :])
                for dst in dsts:
                    last = nc.scalar.activation(dst, psum[0:rows, ln_bank[which][j], 0:SEQ], ACT.Identity,
                                                bias=mod_cur[which][0:rows, 0, j:j + 1],
                                                scale=mod_cur[which][0:rows, 1, j:j + 1])
                last.then_inc(s_xv[which], 1)

            def qkv_read(q, t):
                act.wait_ge(s_qkv, q * TILES + t + 1)
                act.wait_ge(s_qsum, q * TILES)
                nc.scalar.activation(squares[:, t, :].rearrange("p (c n) -> p c n", c=2),
                                     psum[:, 3 * t:3 * t + 2, 0:H], ACT.Square).then_inc(s_sq, 1)
                act.wait_ge(s_pv, q * GROUPS)
                nc.scalar.activation(v_ext[:, t, :, 0:HD], psum[:, 3 * t + 2, 0:H].rearrange("p (h d) -> p h d", d=HD),
                                     ACT.Copy).then_inc(s_v, 1)

            def qk_high(q, t):
                n = q * TILES + t
                act.wait_ge(s_qkn, n + 1)
                act.wait_ge(s_stk, 4 * q)
                for c, src, places in ((1, qk_norm[:, t, H:QK], slice(0, 2)), (0, q_gained[:, t, :], slice(0, 3, 2))):
                    if c == 0:
                        act.wait_ge(s_qg, n + 1)
                    nc.scalar.activation(qk_stack[:, t, c, :, 0:SHIFT].rearrange("p h (r d) -> p h r d", r=3)[:, :, places, :],
                                         src.rearrange("p (h o d) -> p h o d", o=1, d=HD).broadcast_to((P, NH, 2, HD)),
                                         ACT.Copy).then_inc(s_qround, 1)

            def q_read(q, n):
                t, i = n // 2, n % 2
                act.wait_ge(s_stq, 4 * q + n + 1)
                act.wait_ge(s_score, UNITS * q)
                nc.scalar.activation(qT[:, 4 * i:4 * i + 4, t * P:(t + 1) * P],
                                     psum[:, 6, :].rearrange("p (u n) -> p u n", u=4), ACT.Copy).then_inc(s_qT, 1)

            def load_table(function):
                nc.scalar.activation(table_out[:, :], table_in[:, :], function)

            def exp(p, u):
                act.wait_ge(s_score, UNITS * p + u + 1)
                act.wait_ge(s_pv, GROUPS * p + u // 2 - 1 if u >= 4 else GROUPS * p)
                nc.scalar.activation(prob[:, u % 4, :].rearrange("p (c n) -> p c n", c=2),
                                     psum[:, score_bank(u):score_bank(u) + 2, :], ACT.Exp).then_inc(s_exp, 1)

            def o_read(p, t):
                act.wait_ge(s_oback, p * TILES + t + 1)
                act.wait_ge(s_proj, p * TILES)
                nc.scalar.activation(o_stack[:, t, :], psum[:, 6, :], ACT.Copy).then_inc(s_ostack, 1)
                nc.scalar.activation(o_tail[0:TAIL3, t * P:(t + 1) * P], psum[0:TAIL3, 7, 0:P], ACT.Copy).then_inc(s_ostack, 1)

            def gelu(m, i):
                n = SEQ * len(range(2 * i, min(2 * i + 2, FT)))
                act.wait_ge(s_up, MU * m + i + 1)
                act.wait_ge(s_hs, MU * m + i - 1 if i >= 2 else MU * m)
                act.wait_ge(s_down, MU * m + i - 1 if i >= 2 else MU * m)
                for dst in (hidden, hid_hi):
                    last = nc.scalar.activation(dst[:, i % 2, 0:n], psum[:, hidden_bank[i % 2], 0:n], ACT.Gelu_apprx_tanh)
                last.then_inc(s_gelu, 1)

            def round_weights(c, n, s_raw, s_hi):
                cols = slice(c, c + n)
                act.wait_ge(s_raw, 96)
                nc.scalar.activation(w_hi[:, :, cols], raw_w[:, 0:2, cols], ACT.Copy)
                nc.scalar.activation(w_tail[0:TAIL3 + 1, cols], raw_w[0:TAIL3 + 1, 2, cols], ACT.Copy).then_inc(s_hi, 1)

            act.wait_ge(s_bias0, 1)
            round_weights(W_PROJ, H, s_projraw, s_projhi)
            act.wait_ge(s_centred, 1)
            round_weights(W_QKV, 3 * H, s_qkvraw, s_qkvhi)
            round_weights(W_1, MLP, s_w1raw, s_w1hi)
            for j in range(3):
                modulate(0, 0, j)
            act.wait_ge(s_w2raw, 48)
            act.wait_ge(s_const, 2)
            nc.scalar.activation(w2_hi[:, :, :], raw_w2, ACT.Copy)
            nc.scalar.activation(b2_rows[0:1, :], gate2[0:1, :], ACT.Copy).then_inc(s_w2hi, 1)
            qkv_read(0, 0)
            qkv_read(0, 1)
            qk_high(0, 0)
            qk_high(0, 1)
            for n in range(3):
                q_read(0, n)
            for s in (s_wproj, s_w1, s_w2):
                act.wait_ge(s, 1)

            def body(p, more, prev, older):
                for u in range(UNITS):
                    exp(p, u)
                if more:
                    qkv_read(p + 1, 0)
                o_read(p, 0)
                o_read(p, 1)
                if more:
                    qkv_read(p + 1, 1)
                if prev:
                    load_table(ACT.Gelu_apprx_tanh)
                    gelu(p - 1, 0)
                if more:
                    qk_high(p + 1, 0)
                if prev:
                    gelu(p - 1, 1)
                if prev:
                    gelu(p - 1, 2)
                if more:
                    q_read(p + 1, 0)
                    qk_high(p + 1, 1)
                if prev:
                    gelu(p - 1, 3)
                if more:
                    q_read(p + 1, 1)
                if prev:
                    gelu(p - 1, 4)
                if more:
                    q_read(p + 1, 2)
                for j in range(3):
                    modulate(1, p, j)
                load_table(ACT.Exp)

            passes(act, body)
            for i in range(MU):
                gelu(SEQS - 1, i)

        @block.vector
        def _(dve):
            done = 0

            def step(ins):
                nonlocal done
                done += 1
                ins.then_inc(s_setup, 1)

            def layernorm(which, n, src):
                for t in range(TILES):
                    last = nc.vector.bn_stats(ln_stats[:, t, :], src[:, t, :])
                last.then_inc(s_stats[which], 1)
                dve.wait_ge(s_gain, 1)
                dve.wait_ge(s_stats[which], n + 1)
                for t in range(TILES):
                    last = nc.vector.bn_aggr(ln_mv[:, t, :], ln_stats[:, t, :])
                last.then_inc(s_aggr[which], 1)
                dve.wait_ge(s_aggr[which], n + 1)
                nc.vector.tensor_scalar_add(ln_var[:, :], ln_mv[:, :, 1], EPS).then_inc(s_var[which], 1)

            def normalise(which, n, src):
                dve.wait_ge(s_rstd[which], n + 1)
                for t in range(TILES):
                    args = (ln_mv[:, t, 0:1], ln_rstd[:, t:t + 1], ALU.subtract, ALU.mult)
                    nc.vector.tensor_scalar(z[:, t, 0:H], src[:, t, :], *args)
                    last = nc.vector.tensor_scalar(
                        z[:, t, H:ZW].rearrange("p (r n) -> p r n", r=2),
                        src[:, t, 2 * P:H].rearrange("p (o n) -> p o n", o=1).broadcast_to((P, 2, TAIL)), *args)
                last.then_inc(s_z[which], 1)

            def modulate(n, j):
                rows = P if j < 2 else TAIL3
                dve.wait_ge(s_modc[0], n + 1)
                dve.wait_ge(s_zT[0], 3 * n + j + 1)
                dve.wait_ge(s_xs[0], 3 * n)
                dve.wait_ge(s_qkv, TILES * n)
                high = xs_hi[0][:, j, :] if j < 2 else xs_tail[0][0:TAIL3, :]
                for dst in (xv_qkv[0:rows, j, :], high):
                    last = nc.vector.tensor_scalar(dst, psum[0:rows, ln_bank[0][j], 0:SEQ],
                                                   mod_cur[0][0:rows, 1, j:j + 1], mod_cur[0][0:rows, 0, j:j + 1],
                                                   ALU.mult, ALU.add)
                last.then_inc(s_xv[0], 1)

            def round_x2(m):
                dve.wait_ge(s_xv[1], 3 * m + 3)
                dve.wait_ge(s_up, MU * m)
                nc.vector.tensor_copy(xs_hi[1][:, :, :], xv_mlp[:, 0:2, :])
                nc.vector.tensor_copy(xs_tail[1][0:TAIL3, :], xv_mlp[0:TAIL3, 2, :]).then_inc(s_x2round, 1)

            def split_x(which, n, j):
                xv, hi, lo, tail = (xv_qkv, xv_mlp)[which], xs_hi[which], xs_lo[which], xs_tail[which]
                if which == 0:
                    dve.wait_ge(s_xv[0], 3 * n + j + 1)
                else:
                    dve.wait_ge(s_x2round, n + 1)
                if j < 2:
                    nc.vector.tensor_tensor(lo[:, j, :], xv[:, j, :], hi[:, j, :], ALU.subtract).then_inc(s_xs[which], 1)
                else:
                    low = slice(TAIL, 2 * TAIL)
                    nc.vector.tensor_tensor(tail[low, :], xv[low, 2, :], tail[low, :], ALU.subtract).then_inc(s_xs[which], 1)

            def heads(ap):
                return ap.rearrange("p (h d) -> p h d", d=HD)

            def qk_variance(q, t):
                n = q * TILES + t
                dve.wait_ge(s_qvar, n)
                dve.wait_ge(s_sq, n + 1)
                nc.vector.tensor_reduce(qk_sum[:, :], heads(squares[:, t, :]), AX.X, ALU.add).then_inc(s_qsum, 1)
                dve.wait_ge(s_qsum, n + 1)
                dve.wait_ge(s_qrstd, q)
                nc.vector.tensor_scalar(qk_var[:, t, :], qk_sum[:, :], 1.0 / HD, EPS, ALU.mult, ALU.add).then_inc(s_qvar, 1)

            def qk_rsqrt(q):
                var, r = qk_var[:, 0, :], qk_rstd[:, 0, :]
                dve.wait_ge(s_qvar, q * TILES + 1)
                nc.vector.tensor_scalar(r.bitcast(I32), var.bitcast(I32), -0.5, RSQRT_MAGIC, ALU.mult, ALU.add)
                nc.vector.tensor_scalar(half_v[:, :], var, -0.5, None, ALU.mult).then_inc(s_newton_v, 1)
                for i in range(3):
                    steps = q * RSQRT_STEPS_V + 3 * i
                    dve.wait_ge(s_newton_v, steps + 1)
                    nc.vector.tensor_tensor(square_v[:, :], r, r, ALU.mult).then_inc(s_newton_v, 1)
                    dve.wait_ge(s_newton_v, steps + 2)
                    nc.vector.tensor_tensor(square_v[:, :], square_v[:, :], half_v[:, :], ALU.mult).then_inc(s_newton_v, 1)
                    dve.wait_ge(s_newton_v, steps + 3)
                    nc.vector.scalar_tensor_tensor(r, square_v[:, :], 1.5, r, ALU.add, ALU.mult).then_inc(s_newton_v, 1)

            def qk_normalise(q, t):
                n = q * TILES + t
                if t == 0:
                    dve.wait_ge(s_newton_v, (q + 1) * RSQRT_STEPS_V)
                else:
                    dve.wait_ge(s_qrstd, q + 1)
                dve.wait_ge(s_stack, n - t)
                for c, s_done in ((1, None), (0, s_qkn)):
                    last = nc.vector.tensor_tensor(
                        heads(qk_norm[:, t, c * H:(c + 1) * H]), heads(psum[:, 3 * t + c, 0:H]),
                        qk_rstd[:, t, c * NH:(c + 1) * NH].rearrange("p (h o) -> p h o", o=1).broadcast_to((P, NH, HD)), ALU.mult)
                last.then_inc(s_qkn, 1)

            def qk_low(q, t):
                n = q * TILES + t
                dve.wait_ge(s_qround, 2 * n + 2)
                for c, low_at in ((1, 2 * HD), (0, HD)):
                    src = heads(qk_norm[:, t, H:QK] if c else q_gained[:, t, :])
                    last = nc.vector.tensor_tensor(qk_stack[:, t, c, :, low_at:low_at + HD], src,
                                                   qk_stack[:, t, c, :, 0:HD], ALU.subtract)
                last.then_inc(s_stack, 1)

            def k_read(q, n):
                t, i = n // 2, n % 2
                dve.wait_ge(s_stk, 4 * q + n + 1)
                dve.wait_ge(s_score, UNITS * q)
                nc.vector.tensor_copy(kT[:, 4 * i:4 * i + 4, t * P:(t + 1) * P],
                                      psum[:, 7, :].rearrange("p (u n) -> p u n", u=4)).then_inc(s_kT, 1)

            def last_q_read(q):
                dve.wait_ge(s_stq, 4 * q + 4)
                dve.wait_ge(s_score, UNITS * q)
                nc.vector.tensor_copy(qT[:, 4:8, P:2 * P], psum[:, 6, :].rearrange("p (u n) -> p u n", u=4)).then_inc(s_qlast, 1)

            def hand_on(m):
                dve.wait_ge(s_x2, m * TILES + TILES)
                dve.wait_ge(s_y, m * TILES)
                nc.vector.tensor_copy(x2_prev, x2).then_inc(s_x2c, 1)

            def attn_read(p, g):
                dve.wait_ge(s_pv, GROUPS * p + g + 1)
                dve.wait_ge(s_oT, p * TILES)
                nc.vector.tensor_copy(attn[:, g, :], psum[:, 4 + g % 2, 0:SEQ]).then_inc(s_attn, 1)

            def o_normalise(p, t):
                n = p * TILES + t
                of_head = psum[:, 6 + t, :].rearrange("p (h d) -> p h d", d=VW)
                dve.wait_ge(s_oT, n + 1)
                nc.vector.reciprocal(o_recip[:, :], of_head[:, :, HD]).then_inc(s_recip, 1)
                dve.wait_ge(s_recip, n + 1)
                nc.vector.tensor_tensor(heads(o_norm[:, t, :]), of_head[:, :, 0:HD],
                                        o_recip[:, :].rearrange("p (h o) -> p h o", o=1).broadcast_to((P, NH, HD)),
                                        ALU.mult).then_inc(s_on, 1)

            def o_split_tile(p, t):
                n = p * TILES + t
                dve.wait_ge(s_on, n + 1)
                dve.wait_ge(s_oback, p * TILES)
                nc.vector.tensor_copy(o_split[:, t, 0:H], o_norm[:, t, :])
                nc.vector.tensor_copy(o_split[:, t, H + TAIL:ZW], o_norm[:, t, 2 * P:H]).then_inc(s_oround, 1)
                dve.wait_ge(s_oround, n + 1)
                nc.vector.tensor_tensor(o_split[:, t, ZW:OW], o_norm[:, t, 0:2 * P], o_split[:, t, 0:2 * P], ALU.subtract)
                nc.vector.tensor_tensor(o_split[:, t, H:H + TAIL], o_norm[:, t, 2 * P:H], o_split[:, t, 2 * P:H],
                                        ALU.subtract).then_inc(s_os, 1)

            def residual(p, t):
                n = p * TILES + t
                dve.wait_ge(s_proj, n + 1)
                dve.wait_ge(s_g1, 16 * (p + 1))
                dve.wait_ge(s_x2c, p)
                nc.vector.tensor_tensor(x2[:, t, :], psum[:, 6 + t, 0:H], gate1[:, 0, :], ALU.mult).then_inc(s_pg, 1)
                dve.wait_ge(s_pg, n + 1)
                dve.wait_ge(s_xres, 16 * (p + 1))
                nc.vector.tensor_tensor(x2[:, t, :], x2[:, t, :], x_res[:, t, :], ALU.add).then_inc(s_x2, 1)

            def split_hidden(m, i):
                n = SEQ * len(range(2 * i, min(2 * i + 2, FT)))
                dve.wait_ge(s_gelu, MU * m + i + 1)
                dve.wait_ge(s_down, MU * m + i - 1 if i >= 2 else MU * m)
                nc.vector.tensor_tensor(hid_lo[:, i % 2, 0:n], hidden[:, i % 2, 0:n], hid_hi[:, i % 2, 0:n],
                                        ALU.subtract).then_inc(s_hs, 1)

            def output(m):
                dve.wait_ge(s_down, MU * m + MU)
                dve.wait_ge(s_g2, 16 * (m + 1))
                dve.wait_ge(s_x2c, m + 1)
                dve.wait_ge(s_out, 16 * m)
                for t in range(TILES):
                    nc.vector.tensor_tensor(y[:, t, :], psum[:, t, 0:H], gate2[:, :], ALU.mult).then_inc(s_yg, 1)
                for t in range(TILES):
                    dve.wait_ge(s_yg, m * TILES + t + 1)
                    nc.vector.tensor_tensor(y[:, t, :], y[:, t, :], x2_prev[:, t, :], ALU.add).then_inc(s_y, 1)

            nc.vector.memset(w_tail[TAIL3:STACK, :].bitcast(F32), 0.0).then_inc(s_bias0, 1)
            for t in range(TILES):
                nc.vector.memset(qk_stack[:, t, :, :, SHIFT:HALF].bitcast(F32), 0.0)
            nc.vector.memset(v_ext[:, :, :, HD:VW], 0.0)
            nc.vector.memset(mod_all[:, :, :, :], 0.0)
            nc.vector.memset(b2_rows[:, :].bitcast(F32), 0.0)
            nc.vector.memset(ones_r[:, :].bitcast(F32), 1.0)
            nc.vector.memset(table_in[:, :], 0.0)
            for tail in (*xs_tail, o_tail):
                nc.vector.memset(tail[TAIL3:STACK, :].bitcast(F32), 1.0)
            step(nc.vector.memset(silu[KM:KM + 1, :, :], 1.0))
            dve.wait_ge(s_setup, done)
            nc.vector.memset(qk_stack[:, :, 1, :, SHIFT:SROWS].bitcast(F32), 1.0)
            nc.vector.memset(v_ext[:, :, :, HD:HD + 1], 1.0)
            dve.wait_ge(s_ident, 1)
            nc.vector.tensor_copy(ident_r[:, :], ident[:, :]).then_inc(s_const, 1)
            dve.wait_ge(s_tanh, 1)
            step(nc.vector.tensor_scalar(cond_tanh[:, :, :], cond_tanh[:, :, :], 0.5, 0.5, ALU.mult, ALU.add))
            dve.wait_ge(s_setup, done)
            nc.vector.tensor_tensor(silu[0:KM, :, :], cond_tanh[:, :, :], cond[:, :, :], ALU.mult).then_inc(s_silu, 1)
            dve.wait_ge(s_g, 32)
            step(nc.vector.tensor_tensor(gain[:, :], g_both[:, 0, :], g_both[:, 1, :], ALU.mult))
            dve.wait_ge(s_setup, done)
            step(nc.vector.tensor_scalar(gain[:, :], gain[:, :], HD ** -0.5, None, ALU.mult))
            dve.wait_ge(s_setup, done)
            nc.vector.tensor_reduce(bound[:, :], gain[:, :], AX.X, ALU.max, apply_absolute_value=True).then_inc(s_gain, 1)
            dve.wait_ge(s_gain, 1)
            nc.vector.tensor_scalar(flag[:, :], bound[:, :], float(HD), SCORE_BOUND, ALU.mult, ALU.is_gt).then_inc(s_flag, 1)
            dve.wait_ge(s_x, 16)
            layernorm(0, 0, x_ln)
            normalise(0, 0, x_ln)
            dve.wait_ge(s_qkvraw, 96)
            rows_of = (P, P, STACK)
            for k, rows in enumerate(rows_of):
                nc.vector.tensor_reduce(col_mean[0:rows, k, :], heads(raw_w[0:rows, k, 0:QK]), AX.X, ALU.add)
            step(nc.vector.memset(bound[:, :], 0.0))
            dve.wait_ge(s_setup, done)
            for k, rows in enumerate(rows_of):
                last = nc.vector.tensor_scalar(col_mean[0:rows, k, :], col_mean[0:rows, k, :], 1.0 / HD, None, ALU.mult)
            step(last)
            dve.wait_ge(s_setup, done)
            for k, rows in enumerate(rows_of):
                last = nc.vector.tensor_tensor(
                    heads(raw_w[0:rows, k, 0:QK]), heads(raw_w[0:rows, k, 0:QK]),
                    col_mean[0:rows, k, :].rearrange("p (h o) -> p h o", o=1).broadcast_to((rows, 2 * NH, HD)), ALU.subtract)
            last.then_inc(s_centred, 1)
            dve.wait_ge(s_qkvhi, 1)
            low = slice(2 * TAIL, STACK)
            nc.vector.tensor_tensor(w_tail[low, 0:3 * H], raw_w[low, 2, 0:3 * H], w_tail[low, 0:3 * H], ALU.subtract)
            nc.vector.tensor_tensor(w_lo[:, :, 0:3 * H], raw_w[:, 0:2, 0:3 * H], w_hi[:, :, 0:3 * H], ALU.subtract).then_inc(s_wqkv, 1)
            dve.wait_ge(s_modmm, 1)
            cols = psum[:, 7, 0:12 * SEQS].rearrange("p (w k j b) -> p w k j b", w=2, k=2, j=3)
            for rows, j in ((P, 0), (P, 1), (TAIL3, 2)):
                for w in range(2):
                    nc.vector.tensor_copy(mod_all[0:rows, 2 * w, j, :], cols[0:rows, w, 0, j, :])
                    last = nc.vector.tensor_scalar_add(mod_all[0:rows, 2 * w + 1, j, :], cols[0:rows, w, 1, j, :], 1.0)
            last.then_inc(s_mod, 1)
            dve.wait_ge(s_mod, 1)
            nc.vector.tensor_copy(mod_cur[0][:, :, :], mod_all[:, 0:2, :, 0]).then_inc(s_modc[0], 1)
            for j in range(3):
                split_x(0, 0, j)
            dve.wait_ge(s_gatemm, 1)
            nc.vector.tensor_copy(gate_rows[:, :, :], psum[0:SEQS, 4:6, 0:H]).then_inc(s_gate, 1)
            qk_variance(0, 0)
            qk_rsqrt(0)
            qk_variance(0, 1)
            dve.wait_ge(s_w2hi, 1)
            nc.vector.tensor_tensor(w2_lo[:, :, :], raw_w2, w2_hi[:, :, :], ALU.subtract)
            nc.vector.tensor_tensor(b2_rows[0:2, :], gate2[0:2, :], b2_rows[0:2, :], ALU.subtract).then_inc(s_w2, 1)
            for t in range(TILES):
                qk_normalise(0, t)
            for t in range(TILES):
                qk_low(0, t)
            for n in range(4):
                if n == 3:
                    last_q_read(0)
                k_read(0, n)
            for s in (s_wproj, s_w1):
                dve.wait_ge(s, 1)
            needs_shift = dve.value_load(flag[0:1, 0:1], min_val=0, max_val=1)

            def body(p, more, prev, older):
                if more:
                    dve.wait_ge(s_x, 16 * (p + 2))
                    layernorm(0, p + 1, x_ln)
                if older:
                    output(p - 2)
                with dve.If(needs_shift > 0):
                    for n in range(TILES * GROUPS):
                        t, g = n // GROUPS, n % GROUPS
                        dve.wait_ge(s_ms, TILES * GROUPS * p + n + 1)
                        two = 2 * (n % 2)
                        nc.vector.tensor_reduce(
                            neg_max[:, t, :].rearrange("p (j u) -> p j u", j=2)[:, :, 2 * g:2 * g + 2],
                            psum[:, two:two + 2, :].rearrange("p j (u n) -> p j u n", u=2),
                            AX.X, ALU.max, negate=True).then_inc(s_mx, 1)
                    dve.wait_ge(s_mT, p + 1)
                    dve.wait_ge(s_md, 32 * p)
                    nc.vector.tensor_copy(shiftT[:, :], psum[0:NH, 4, 0:SEQ]).then_inc(s_mc, 1)
                if more:
                    dve.wait_ge(s_zT[1], 3 * p)
                    normalise(0, p + 1, x_ln)
                attn_read(p, 0)
                if prev:
                    hand_on(p - 1)
                if more:
                    modulate(p + 1, 0)
                    modulate(p + 1, 1)
                attn_read(p, 1)
                if more:
                    split_x(0, p + 1, 0)
                    split_x(0, p + 1, 1)
                    modulate(p + 1, 2)
                attn_read(p, 2)
                if more:
                    split_x(0, p + 1, 2)
                if prev:
                    round_x2(p - 1)
                attn_read(p, 3)
                for t in range(TILES):
                    o_normalise(p, t)
                    o_split_tile(p, t)
                if prev:
                    for j in range(3):
                        split_x(1, p - 1, j)
                if more:
                    qk_variance(p + 1, 0)
                    qk_rsqrt(p + 1)
                    qk_normalise(p + 1, 0)
                    qk_variance(p + 1, 1)
                if prev:
                    split_hidden(p - 1, 0)
                residual(p, 0)
                residual(p, 1)
                if more:
                    qk_low(p + 1, 0)
                if prev:
                    split_hidden(p - 1, 1)
                if more:
                    qk_normalise(p + 1, 1)
                dve.wait_ge(s_x2, p * TILES + TILES)
                layernorm(1, p, x2)
                if prev:
                    split_hidden(p - 1, 2)
                if more:
                    k_read(p + 1, 0)
                    qk_low(p + 1, 1)
                    dve.wait_ge(s_zT[0], 3 * (p + 2))
                else:
                    dve.wait_ge(s_zT[0], 3 * (p + 1))
                normalise(1, p, x2)
                if prev:
                    split_hidden(p - 1, 3)
                if more:
                    k_read(p + 1, 1)
                if prev:
                    split_hidden(p - 1, 4)
                if more:
                    k_read(p + 1, 2)
                if more:
                    last_q_read(p + 1)
                    k_read(p + 1, 3)

            passes(dve, body)
            output(SEQS - 2)
            hand_on(SEQS - 1)
            round_x2(SEQS - 1)
            for j in range(3):
                split_x(1, SEQS - 1, j)
            for i in range(MU):
                split_hidden(SEQS - 1, i)
            output(SEQS - 1)


def kernel(x, cond_1152, L0_cond_w_mod, L0_cond_b_mod, L0_cond_w_qkv, L0_cond_b_qkv, L0_cond_g_q, L0_cond_g_k,
           L0_cond_w_proj, L0_cond_b_proj, L0_cond_w1, L0_cond_b1, L0_cond_w2, L0_cond_b2):
    import numpy as np
    from concourse import bacc
    from concourse.bass_utils import run_bass_kernel_spmd

    arrays = {"x": x, "condT": np.asarray(cond_1152).T, "w_mod": L0_cond_w_mod, "b_mod": L0_cond_b_mod,
              "w_qkv": L0_cond_w_qkv, "b_qkv": L0_cond_b_qkv, "g_q": L0_cond_g_q, "g_k": L0_cond_g_k,
              "w_proj": L0_cond_w_proj, "b_proj": L0_cond_b_proj, "w1": L0_cond_w1, "b1": L0_cond_b1,
              "w2": L0_cond_w2, "b2": L0_cond_b2}
    nc = bacc.Bacc("TRN2", target_bir_lowering=False, num_devices=1)
    feeds, args = {}, []
    for name, a in arrays.items():
        a = np.ascontiguousarray(a)
        feeds[f"in_{name}"] = a
        args.append(nc.dram_tensor(f"in_{name}", a.shape, mybir.dt.from_np(a.dtype), kind="ExternalInput").ap())
    args.append(nc.dram_tensor("gate_scratch", (SEQS, 2 * H), F32, kind="Internal").ap())
    args.append(nc.dram_tensor("out_0", x.shape, F32, kind="ExternalOutput").ap())
    dit_block(nc, *args)
    r = run_bass_kernel_spmd(nc, [feeds], core_ids=[0])
    return r.results[0]["out_0"]
```

```python
from contextlib import ExitStack

import concourse.bass as bass
from concourse import mybir

F32 = mybir.dt.float32
F32R = mybir.dt.float32r
I32 = mybir.dt.int32
ACT = mybir.ActivationFunctionType
ALU = mybir.AluOpType
AX = mybir.AxisListType

P = 128
SEQS, SEQ, H = 8, 256, 288
NH = 16
HD = H // NH
MLP = 4 * H
TILES = SEQ // P
UNITS = NH // 2
GROUPS = NH // 4
FT = MLP // P
MU = (FT + 1) // 2
TAIL = H - 2 * P
TAIL3 = 3 * TAIL
STACK = TAIL3 + 2
ZW = 2 * P + TAIL3
OW = ZW + 2 * P
KM = H // 3
HALF = 64
SHIFT = 3 * HD
SROWS = SHIFT + 1
VW = 32
NMOD = 6 * H
EPS = 1e-6
SCORE_BOUND = 60.0
RSQRT_MAGIC = float(0x5F3759DF)
RSQRT_STEPS_V = 10
RSQRT_STEPS = 12
W_QKV, W_PROJ, W_1 = 0, 3 * H, 4 * H
W_ALL = 4 * H + MLP
QK = 2 * H


def dit_block(nc, x, condT, w_mod, b_mod, w_qkv, b_qkv, g_q, g_k, w_proj, b_proj, w1, b1, w2, b2,
              gate_scratch, out):
    x_seqs = x.rearrange("s (t p) f -> s p t f", p=P)
    out_seqs = out.rearrange("s (t p) f -> s p t f", p=P)

    with ExitStack() as ctx:
        def sb(name, shape, dt=F32):
            return ctx.enter_context(nc.sbuf_tensor(name, shape, dt))

        def sem(name):
            return ctx.enter_context(nc.semaphore(name))

        w_hi = sb("w_hi", [P, 2, W_ALL], F32R)
        w_lo = sb("w_lo", [P, 2, W_ALL], F32R)
        w_tail = sb("w_tail", [STACK, W_ALL], F32R)
        w2_hi = sb("w2_hi", [P, FT, H], F32R)
        w2_lo = sb("w2_lo", [P, FT, H], F32R)
        b2_rows = sb("b2_rows", [P, H], F32R)
        arena = sb("arena", [P, 3 * W_ALL + 3 * NMOD + FT * H])
        raw_w = arena[:, 0:3 * W_ALL].rearrange("p (k n) -> p k n", k=3)
        raw_mod = arena[:, 3 * W_ALL:3 * W_ALL + 3 * NMOD].rearrange("p (k n) -> p k n", k=3)
        raw_w2 = arena[:, 3 * W_ALL + 3 * NMOD:].rearrange("p (k n) -> p k n", k=FT)

        def carve(start, *shape):
            size = shape[0] * shape[1]
            return arena[:, start:start + size].rearrange("p (u n) -> p u n", u=shape[0]), start + size

        at = 0
        prob, at = carve(at, 4, 4 * SEQ)
        o_norm, at = carve(at, TILES, H)
        xv_mlp, at = carve(at, 3, SEQ)
        attn, at = carve(at, GROUPS, SEQ)
        assert at <= 3 * W_ALL
        squares = raw_w[:, 0:TILES, 0:QK]
        qk_norm = raw_mod[:, 0:TILES, 0:QK]
        q_gained = raw_mod[:, TILES, 0:TILES * H].rearrange("p (t n) -> p t n", t=TILES)
        hidden = raw_mod[:, 0:2, 3 * H:3 * H + 2 * SEQ]
        at = 3 * W_ALL + 3 * NMOD
        y, at = carve(at, TILES, H)
        x2_prev, at = carve(at, TILES, H)
        x2, at = carve(at, TILES, H)
        x_res, at = carve(at, TILES, H)
        gate1, at = carve(at, 1, H)
        assert at <= 3 * W_ALL + 3 * NMOD + FT * H
        x_ln = sb("x_ln", [P, TILES, H])
        z = sb("z", [P, TILES, ZW])
        xv_qkv = sb("xv_qkv", [P, 3, SEQ])
        gate2 = sb("gate2", [P, H])
        xs_hi = [sb(f"xs_hi_{n}", [P, 2, SEQ], F32R) for n in ("qkv", "mlp")]
        xs_lo = [sb(f"xs_lo_{n}", [P, 2, SEQ], F32R) for n in ("qkv", "mlp")]
        xs_tail = [sb(f"xs_tail_{n}", [STACK, SEQ], F32R) for n in ("qkv", "mlp")]
        o_split = sb("o_split", [P, TILES, OW], F32R)
        o_stack = sb("o_stack", [P, TILES, 4 * P], F32R)
        o_tail = sb("o_tail", [STACK, SEQ], F32R)
        qk_stack = sb("qk_stack", [P, TILES, 2, NH, HALF], F32R)
        qT = sb("qT", [P, UNITS, SEQ], F32R)
        kT = sb("kT", [P, UNITS, SEQ], F32R)
        v_ext = sb("v_ext", [P, TILES, NH, VW])
        hid_hi = sb("hid_hi", [P, 2, 2 * SEQ], F32R)
        hid_lo = sb("hid_lo", [P, 2, 2 * SEQ], F32R)
        ident = sb("ident", [P, P])
        ident_r = sb("ident_r", [P, P], F32R)
        ones_r = sb("ones_r", [P, P], F32R)
        cond = sb("cond", [KM, 3, SEQS])
        cond_tanh = sb("cond_tanh", [KM, 3, SEQS])
        silu = sb("silu", [KM + 1, 3, SEQS])
        mod_all = sb("mod_all", [P, 4, 3, SEQS])
        mod_cur = [sb(f"mod_cur_{n}", [P, 2, 3]) for n in ("qkv", "mlp")]
        gate_rows = sb("gate_rows", [SEQS, 2, H])
        col_mean = sb("col_mean", [P, 3, 2 * NH])
        both = ("qkv", "mlp")
        g_both = sb("g_both", [P, 2, HD])
        gain = sb("gain", [P, HD])
        bound = sb("bound", [P, 1])
        flag = sb("flag", [P, 1], I32)
        minus_half = sb("minus_half", [P, 2 * NH])
        three_halves = sb("three_halves", [P, 2 * NH])
        table_in = sb("table_in", [P, 1])
        table_out = sb("table_out", [P, 1])
        ln_stats = [sb(f"ln_stats_{n}", [P, TILES, 6]) for n in both]
        ln_mv = [sb(f"ln_mv_{n}", [P, TILES, 2]) for n in both]
        ln_var = [sb(f"ln_var_{n}", [P, TILES]) for n in both]
        ln_rstd = [sb(f"ln_rstd_{n}", [P, TILES]) for n in both]
        qk_sum = sb("qk_sum", [P, 2 * NH])
        qk_var = sb("qk_var", [P, TILES, 2 * NH])
        half_v, qk_half = sb("half_v", [P, 2 * NH]), sb("qk_half", [P, 2 * NH])
        square_v, qk_square = sb("square_v", [P, 2 * NH]), sb("qk_square", [P, 2 * NH])
        qk_rstd = sb("qk_rstd", [P, TILES, 2 * NH])
        o_recip = sb("o_recip", [P, NH])
        neg_max = sb("neg_max", [P, TILES, NH])
        shiftT = sb("shiftT", [NH, SEQ])

        psum = ctx.enter_context(nc.psum_tensor("psum", [P, 8, 512], F32))
        hidden_bank = (2, 5)

        def score_bank(u):
            return 4 if u == 1 else 2 if u % 2 == 0 else 0

        mod_bank = (5, 3)

        def ln_bank(which, n):
            return (4, 5, 3) if which else (6, 7, 4) if isinstance(n, int) and n == 0 else (6, 7, 6)


        s_const = sem("constants_made")
        s_ident0, s_ident = sem("identity_zeroed"), sem("identity_ready")
        s_cond, s_g = sem("cond_loaded"), sem("gains_loaded")
        s_modraw, s_qkvraw, s_projraw, s_w1raw, s_w2raw = (sem(f"{n}_loaded") for n in ("w_mod", "w_qkv", "w_proj", "w1", "w2"))
        s_setup, s_bias0 = sem("vector_setup_step"), sem("bias_rows_zeroed")
        s_centred, s_low = sem("w_qkv_centred"), sem("full_tiles_low_halves")
        s_qkvhi, s_projhi, s_w1hi, s_w2hi = (sem(f"{n}_rounded") for n in ("w_qkv", "w_proj", "w1", "w2"))
        s_modrest, s_w1tail = sem("w_mod_rest_loaded"), sem("w1_tail_split")
        s_wqkv, s_wproj, s_w1, s_w2 = (sem(f"{n}_split") for n in ("w_qkv", "w_proj", "w1", "w2"))
        s_tanh, s_silu = sem("tanh_done"), sem("silu_ready")
        s_modmm, s_gatemm = sem("mod_products_done"), sem("gate_products_done")
        s_mod, s_gate, s_stored = sem("mod_columns_ready"), sem("gate_rows_ready"), sem("gate_rows_stored")
        s_gain, s_flag = sem("gain_ready"), sem("flag_ready")
        s_x, s_xres, s_g1, s_g2 = sem("x_loaded"), sem("x_res_loaded"), sem("gate1_loaded"), sem("gate2_loaded")
        s_stats = [sem(f"ln_stats_{n}") for n in both]
        s_aggr = [sem(f"ln_aggregated_{n}") for n in both]
        s_var = [sem(f"ln_variance_{n}") for n in both]
        s_rstd = [sem(f"ln_rstd_{n}") for n in both]
        s_z = [sem(f"z_ready_{n}") for n in both]
        s_modc = [sem(f"mod_copied_{n}") for n in both]
        s_zT = [sem(f"z_transposed_{n}") for n in both]
        s_xv = [sem(f"x_modulated_{n}") for n in both]
        s_x2round = sem("x_rounded_mlp")
        s_xs = [sem(f"x_split_{n}") for n in both]
        s_qkv = sem("qkv_done")
        s_sq, s_v = sem("squares_done"), sem("v_read")
        s_qsum, s_qvar, s_qrstd = sem("square_sums_done"), sem("qk_variance"), sem("qk_rstd_ready")
        s_newton_v, s_newton = sem("vector_newton_step"), sem("pool_newton_step")
        s_qkn, s_qg = sem("qk_normalised"), sem("q_gained_ready")
        s_qround, s_stack = sem("qk_rounded"), sem("qk_stack_ready")
        s_st, s_stq, s_stk = sem("stack_tile_done"), sem("q_stack_transposed"), sem("k_stack_transposed")
        s_qT, s_qlast, s_kT = sem("qT_written"), sem("last_qT_written"), sem("kT_written")
        s_score, s_exp = sem("scores_done"), sem("exp_done")
        s_pv, s_attn = sem("attn_group_done"), sem("attn_group_read")
        s_oT, s_recip, s_on = sem("attn_transposed"), sem("row_sums_inverted"), sem("o_normalised")
        s_oround, s_os = sem("o_rounded"), sem("o_split_ready")
        s_oback, s_ostack = sem("o_transposed"), sem("o_stack_written")
        s_proj, s_pg, s_x2 = sem("proj_done"), sem("proj_gated"), sem("x2_ready")
        s_x2c = sem("x2_handed_on")
        s_up, s_gelu = sem("mlp_up_done"), sem("gelu_done")
        s_hs, s_down = sem("hidden_split"), sem("mlp_down_done")
        s_yg, s_y, s_out = sem("mlp_gated"), sem("y_ready"), sem("y_stored")
        s_ms, s_mx = sem("shift_scores_done"), sem("shift_maxima_done")
        s_mT, s_mc, s_md = sem("maxima_transposed"), sem("maxima_copied"), sem("shift_rows_written")

        block = ctx.enter_context(nc.Block())

        def passes(engine, body):
            body(0, True, True, False, False)
            body(1, True, True, True, False)
            with engine.Fori(2, SEQS - 2) as p:
                body(p, True, True, True, True)
            body(SEQS - 2, False, True, True, True)
            body(SEQS - 1, False, False, True, True)

        def dense(pe, dst, hi, lo, tail, cols, act_moves):
            terms = [(hi(0), w_hi[:, 0, cols]), (hi(1), w_hi[:, 1, cols]),
                     (hi(0), w_lo[:, 0, cols]), (hi(1), w_lo[:, 1, cols]),
                     (lo(0), w_hi[:, 0, cols]), (lo(1), w_hi[:, 1, cols]),
                     (tail, w_tail[:, cols])]
            for n, (a, w) in enumerate(terms):
                lhsT, rhs = (w, a) if act_moves else (a, w)
                last = nc.tensor.matmul(dst, lhsT, rhs, start=(n == 0), stop=(n == len(terms) - 1))
            return last

        @block.sync
        def _(sp):
            def row(v):
                return v.rearrange("(o n) -> o n", o=1)

            sp.dma_start(cond[:, :, :], condT.rearrange("(k p) b -> p k b", p=KM)).then_inc(s_cond, 16)
            for i, g in enumerate((g_q, g_k)):
                sp.dma_start(g_both[:, i, :], row(g).broadcast_to((P, HD))).then_inc(s_g, 16)
            sp.dma_start(x_ln[:, :, :], x_seqs[0]).then_inc(s_x, 16)
            w_mod_tiles = w_mod.rearrange("(k p) n -> p k n", p=KM)
            sp.dma_start(raw_mod[0:KM, :, 0:2 * H], w_mod_tiles[:, :, 0:2 * H]).then_inc(s_modraw, 16)
            sp.dma_start(raw_mod[KM:KM + 1, 2, :], row(b_mod)).then_inc(s_modraw, 16)
            for w, b, c, s in ((w_qkv, b_qkv, W_QKV, s_qkvraw), (w_proj, b_proj, W_PROJ, s_projraw), (w1, b1, W_1, s_w1raw)):
                n = w.shape[1]
                sp.dma_start(raw_w[:, 0:2, c:c + n], w[0:2 * P, :].rearrange("(k p) n -> p k n", p=P)).then_inc(s, 16)
                for r in range(3):
                    sp.dma_start(raw_w[r * TAIL:(r + 1) * TAIL, 2, c:c + n], w[2 * P:H, :]).then_inc(s, 16)
                for r in range(2):
                    sp.dma_start(raw_w[TAIL3 + r:TAIL3 + r + 1, 2, c:c + n], row(b)).then_inc(s, 16)
                if w is w_qkv:
                    sp.dma_start(raw_mod[0:KM, :, 2 * H:NMOD], w_mod_tiles[:, :, 2 * H:NMOD]).then_inc(s_modrest, 16)
            sp.dma_start(raw_w2, w2.rearrange("(k p) n -> p k n", p=P)).then_inc(s_w2raw, 16)
            for r in range(2):
                sp.dma_start(gate2[r:r + 1, :], row(b2)).then_inc(s_w2raw, 16)
            sp.wait_ge(s_z[0], 1)
            sp.dma_start(x_ln[:, :, :], x_seqs[1]).then_inc(s_x, 16)
            sp.wait_ge(s_gate, 1)
            sp.dma_start(gate_scratch, gate_rows[:, :, :].rearrange("b g f -> b (g f)")).then_inc(s_stored, 16)
            sp.wait_ge(s_stored, 16)
            sp.wait_ge(s_flag, 1)
            needs_shift = sp.value_load(flag[0:1, 0:1], min_val=0, max_val=1)
            for s in (s_wproj, s_w1, s_w1tail, s_w2):
                sp.wait_ge(s, 1)

            def body(p, further, more, prev, older):
                if further:
                    sp.wait_ge(s_z[0], p + 2)
                    sp.dma_start(x_ln[:, :, :], x_seqs[p + 2]).then_inc(s_x, 16)
                sp.wait_ge(s_x2, p * TILES)
                sp.dma_start(x_res[:, :, :], x_seqs[p]).then_inc(s_xres, 16)
                sp.wait_ge(s_pg, p * TILES)
                sp.dma_start(gate1[:, 0, :], gate_scratch[bass.ds(p, 1), 0:H].broadcast_to((P, H))).then_inc(s_g1, 16)
                if prev:
                    load_gate2(p - 1)
                with sp.If(needs_shift > 0):
                    sp.wait_ge(s_mc, p + 1)
                    for j in range(2):
                        at_row = HALF * j + SHIFT
                        sp.dma_start(qT[at_row:at_row + 1, :, :].bitcast(F32),
                                     shiftT[UNITS * j:UNITS * (j + 1), :]).then_inc(s_md, 16)
                if older:
                    store(p - 2)

            def load_gate2(m):
                sp.wait_ge(s_yg, m * TILES)
                sp.dma_start(gate2[:, :], gate_scratch[bass.ds(m, 1), H:2 * H].broadcast_to((P, H))).then_inc(s_g2, 16)

            def store(m):
                sp.wait_ge(s_y, m * TILES + TILES)
                sp.dma_start(out_seqs[m], y[:, :, :]).then_inc(s_out, 16)

            passes(sp, body)
            store(SEQS - 2)
            load_gate2(SEQS - 1)
            store(SEQS - 1)
            sp.wait_ge(s_out, 16 * SEQS)

        @block.gpsimd
        def _(pool):
            nc.gpsimd.memset(ident[:, :], 0.0).then_inc(s_ident0, 1)
            nc.gpsimd.memset(three_halves[:, :], 1.5)
            nc.gpsimd.memset(minus_half[:, :], -0.5).then_inc(s_const, 1)
            pool.wait_ge(s_ident0, 1)
            nc.gpsimd.affine_select(out=ident[:, :], in_=ident[:, :], compare_op=ALU.not_equal, fill=1.0, base=0,
                                    pattern=[[-1, P]], channel_multiplier=1).then_inc(s_ident, 1)

            def power(s_in, s_result, dst, src, n):
                pool.wait_ge(s_in, n)
                nc.gpsimd.tensor_tensor(dst, src, minus_half[:, 0:src.shape[1]], ALU.pow).then_inc(s_result, 1)

            def ln_power(which, n):
                power(s_var[which], s_rstd[which], ln_rstd[which][:, :], ln_var[which][:, :], n + 1)

            def copy_mod(which, n):
                pool.wait_ge(s_mod, 2)
                pool.wait_ge(s_xv[which], 3 * n)
                nc.gpsimd.tensor_copy(mod_cur[which][:, :, :], mod_all[:, 2 * which:2 * which + 2, :, n]).then_inc(s_modc[which], 1)

            def qk_rsqrt(q):
                steps = (q - 1) * RSQRT_STEPS
                var, r = qk_var[:, 1, :], qk_rstd[:, 1, :]
                pool.wait_ge(s_qvar, q * TILES + 2)
                pool.wait_ge(s_qkn, q * TILES)
                nc.gpsimd.tensor_tensor(qk_half[:, :], var, minus_half[:, :], ALU.mult)
                nc.gpsimd.tensor_scalar(r.bitcast(I32), var.bitcast(I32), -0.5, RSQRT_MAGIC, ALU.mult, ALU.add).then_inc(s_newton, 1)
                for i in range(3):
                    pool.wait_ge(s_newton, steps + 4 * i + 1)
                    nc.gpsimd.tensor_tensor(qk_square[:, :], r, r, ALU.mult).then_inc(s_newton, 1)
                    pool.wait_ge(s_newton, steps + 4 * i + 2)
                    nc.gpsimd.tensor_tensor(qk_square[:, :], qk_square[:, :], qk_half[:, :], ALU.mult).then_inc(s_newton, 1)
                    pool.wait_ge(s_newton, steps + 4 * i + 3)
                    nc.gpsimd.tensor_tensor(qk_square[:, :], qk_square[:, :], three_halves[:, :], ALU.add).then_inc(s_newton, 1)
                    pool.wait_ge(s_newton, steps + 4 * i + 4)
                    last = nc.gpsimd.tensor_tensor(r, r, qk_square[:, :], ALU.mult)
                    if i < 2:
                        last.then_inc(s_newton, 1)
                last.then_inc(s_qrstd, 1)

            def qk_gain(q, t):
                n = q * TILES + t
                pool.wait_ge(s_qkn, n + 1)
                nc.gpsimd.tensor_tensor(
                    q_gained[:, t, :].rearrange("p (h d) -> p h d", d=HD),
                    qk_norm[:, t, 0:H].rearrange("p (h d) -> p h d", d=HD),
                    gain[:, :].rearrange("p (o d) -> p o d", o=1).broadcast_to((P, NH, HD)), ALU.mult).then_inc(s_qg, 1)

            pool.wait_ge(s_const, 2)
            ln_power(0, 0)
            proj, mlp, low = slice(W_PROJ, W_PROJ + H), slice(W_1, W_1 + MLP), slice(2 * TAIL, STACK)
            pool.wait_ge(s_projhi, 1)
            nc.gpsimd.tensor_tensor(w_lo[:, :, proj], raw_w[:, 0:2, proj], w_hi[:, :, proj], ALU.subtract).then_inc(s_low, 1)
            pool.wait_ge(s_low, 1)
            nc.gpsimd.tensor_tensor(w_tail[low, proj], raw_w[low, 2, proj], w_tail[low, proj], ALU.subtract).then_inc(s_wproj, 1)
            pool.wait_ge(s_wproj, 1)
            pool.wait_ge(s_w1hi, 1)
            nc.gpsimd.tensor_tensor(w_lo[:, :, mlp], raw_w[:, 0:2, mlp], w_hi[:, :, mlp], ALU.subtract).then_inc(s_w1, 1)
            pool.wait_ge(s_gain, 1)
            for t in range(TILES):
                qk_gain(0, t)
            ln_power(0, 1)

            def body(p, further, more, prev, older):
                if more:
                    copy_mod(0, p + 1)
                    qk_gain(p + 1, 0)
                    qk_rsqrt(p + 1)
                    qk_gain(p + 1, 1)
                if further:
                    ln_power(0, p + 2)
                ln_power(1, p)
                copy_mod(1, p)

            passes(pool, body)

        @block.tensor
        def _(pe):
            pe.wait_ge(s_silu, 1)
            pe.wait_ge(s_modraw, 32)
            def mod_product(dst, lhs, rhs):
                for k in range(3):
                    rows = KM + (k == 2)
                    last = nc.tensor.matmul(dst, lhs(k, rows), rhs(k, rows), start=(k == 0), stop=(k == 2))
                return last

            def mod_columns(bank, which):
                for i in range(2):
                    for j in range(3):
                        parts = [(0, P, j * P)] if j < 2 else [(r * TAIL, TAIL, 2 * P) for r in range(3)]
                        for row0, m, col0 in parts:
                            at, col = (3 * i + j) * SEQS, (3 * which + i) * H + col0
                            last = mod_product(psum[row0:row0 + m, bank, at:at + SEQS],
                                               lambda k, rows: raw_mod[0:rows, k, col:col + m],
                                               lambda k, rows: silu[0:rows, k, :])
                last.then_inc(s_modmm, 1)

            def ln_transpose(which, n, j):
                pe.wait_ge(s_z[which], n + 1)
                rows = P if j < 2 else TAIL3
                for t in range(TILES):
                    last = nc.tensor.transpose(psum[0:rows, ln_bank(which, n)[j], t * P:(t + 1) * P],
                                               z[:, t, j * P:j * P + rows], ident[:, :])
                last.then_inc(s_zT[which], 1)

            def qkv(q, t, parts=(2, 0, 1)):
                pe.wait_ge(s_xs[0], 3 * q + 3)
                tok = slice(t * P, (t + 1) * P)
                for c in parts:
                    last = dense(pe, psum[:, 3 * t + c, 0:H], lambda k: xs_hi[0][:, k, tok],
                                 lambda k: xs_lo[0][:, k, tok], xs_tail[0][:, tok],
                                 slice(W_QKV + c * H, W_QKV + (c + 1) * H), False)
                if parts[-1] == 1:
                    last.then_inc(s_qkv, 1)

            def stack_transpose(q, n):
                t, i = n // 2, n % 2
                pe.wait_ge(s_stack, q * TILES + t + 1)
                for c, s_done, read in ((0, s_stq, (s_qT, 3 * q + n)), (1, s_stk, (s_kT, 4 * q + n))):
                    if n > 0:
                        pe.wait_ge(*read)
                    for k in range(4):
                        u = 4 * i + k
                        last = nc.tensor.transpose(
                            psum[:, 6 + c, k * P:(k + 1) * P].bitcast(F32R),
                            qk_stack[:, t, c, 2 * u:2 * u + 2, :].rearrange("p h r -> p (h r)"), ident_r[:, :])
                    last.then_inc(s_done, 1)

            def scores(p, u):
                if u % 4 == 0:
                    pe.wait_ge(s_kT, 4 * p + 3 + u // 4)
                if u == 0:
                    pe.wait_ge(s_qT, 3 * p + 3)
                if u == 4:
                    pe.wait_ge(s_qlast, p + 1)
                if u == 2 or u >= 4:
                    pe.wait_ge(s_exp, UNITS * p + u - 1)
                two = score_bank(u)
                for kt in range(TILES):
                    for j in range(2):
                        rows = slice(HALF * j, HALF * j + SROWS)
                        last = nc.tensor.matmul(psum[:, two + j, kt * SEQ:(kt + 1) * SEQ],
                                                kT[rows, u, kt * P:(kt + 1) * P], qT[rows, u, :],
                                                start=True, stop=True)
                last.then_inc(s_score, 1)

            def values(p, g):
                pe.wait_ge(s_exp, UNITS * p + 2 * g + 2)
                if g >= 2:
                    pe.wait_ge(s_attn, GROUPS * p + g - 1)
                for kt in range(TILES):
                    for c in range(4):
                        u, j = 2 * g + c // 2, c % 2
                        last = nc.tensor.matmul(
                            psum[32 * c:32 * c + 32, 4 + g % 2, 0:SEQ], v_ext[:, kt, 4 * g + c, :],
                            prob[:, u % 4, j * 2 * SEQ + kt * SEQ:j * 2 * SEQ + (kt + 1) * SEQ],
                            start=(kt == 0), stop=(kt == TILES - 1))
                last.then_inc(s_pv, 1)

            def o_back(p, t):
                pe.wait_ge(s_os, p * TILES + t + 1)
                if t == 0:
                    pe.wait_ge(s_on, p * TILES + TILES)
                else:
                    pe.wait_ge(s_ostack, 4 * p + 2 * t)
                for i, c in enumerate((0, P, ZW, ZW + P)):
                    nc.tensor.transpose(psum[:, 6, i * P:(i + 1) * P].bitcast(F32R), o_split[:, t, c:c + P], ident_r[:, :])
                nc.tensor.transpose(psum[0:TAIL3, 7, 0:P].bitcast(F32R), o_split[:, t, 2 * P:ZW],
                                    ident_r[:, :]).then_inc(s_oback, 1)

            def project(p, t):
                pe.wait_ge(s_ostack, 4 * p + 4)
                dense(pe, psum[:, 6 + t, 0:H], lambda k: o_stack[:, t, k * P:(k + 1) * P],
                      lambda k: o_stack[:, t, (2 + k) * P:(3 + k) * P], o_tail[:, t * P:(t + 1) * P],
                      slice(W_PROJ, W_PROJ + H), False).then_inc(s_proj, 1)

            def unit_tiles(i):
                return range(2 * i, min(2 * i + 2, FT))

            def up(m, i):
                if i >= 2:
                    pe.wait_ge(s_gelu, MU * m + i - 1)
                for f in unit_tiles(i):
                    last = dense(pe, psum[:, hidden_bank[i % 2], (f % 2) * SEQ:(f % 2 + 1) * SEQ],
                                 lambda k: xs_hi[1][:, k, :], lambda k: xs_lo[1][:, k, :], xs_tail[1][:, :],
                                 slice(W_1 + f * P, W_1 + (f + 1) * P), True)
                last.then_inc(s_up, 1)

            def down(m, i):
                pe.wait_ge(s_hs, MU * m + i + 1)
                for t in range(TILES):
                    if i == 0:
                        nc.tensor.matmul(psum[:, t, 0:H], ones_r[:, :], b2_rows[:, :], start=True, stop=False)
                    for f in unit_tiles(i):
                        tok = slice((f % 2) * SEQ + t * P, (f % 2) * SEQ + (t + 1) * P)
                        for n, (a, w) in enumerate(((hid_hi, w2_hi), (hid_hi, w2_lo), (hid_lo, w2_hi))):
                            last = nc.tensor.matmul(psum[:, t, 0:H], a[:, i % 2, tok], w[:, f, :],
                                                    start=False, stop=(f == FT - 1 and n == 2))
                last.then_inc(s_down, 1)

            def mlp(m, banks_read, between, behind, started=False):
                pe.wait_ge(s_xs[1], 3 * m + 3)
                if not started:
                    up(m, 0)
                between()
                if not started:
                    up(m, 1)
                if banks_read is not None:
                    pe.wait_ge(*banks_read)
                for i in range(MU - 1):
                    down(m, i)
                    if i + 2 < MU:
                        up(m, i + 2)
                    behind(i)

            mod_columns(mod_bank[0], 0)
            pe.wait_ge(s_ident, 1)
            for j in range(3):
                ln_transpose(0, 0, j)
            pe.wait_ge(s_modrest, 16)
            mod_columns(mod_bank[1], 1)
            pe.wait_ge(s_wqkv, 1)
            qkv(0, 0)
            pe.wait_ge(s_mod, 2)
            qkv(0, 1)
            for i, kind in enumerate((2, 5)):
                last = mod_product(psum[0:SEQS, 6 + i, 0:H], lambda k, rows: silu[0:rows, k, :],
                                   lambda k, rows: raw_mod[0:rows, k, kind * H:(kind + 1) * H])
            last.then_inc(s_gatemm, 1)
            pe.wait_ge(s_gate, 1)
            pe.wait_ge(s_xv[0], 3)
            pe.wait_ge(s_const, 2)
            for n in range(4):
                stack_transpose(0, n)
            pe.wait_ge(s_flag, 1)
            needs_shift = pe.value_load(flag[0:1, 0:1], min_val=0, max_val=1)

            def body(p, further, more, prev, older):
                pe.wait_ge(s_v, p * TILES + TILES)
                pe.wait_ge(s_qkn, p * TILES + TILES)
                if prev:
                    pe.wait_ge(s_xv[1], 3 * p)
                if older:
                    pe.wait_ge(s_gelu, (p - 1) * MU)

                def finish():
                    if older:
                        down(p - 2, MU - 1)

                with pe.If(needs_shift > 0):
                    finish()
                    if older:
                        pe.wait_ge(s_yg, (p - 1) * TILES)
                    pe.wait_ge(s_qT, 3 * p + 3)
                    pe.wait_ge(s_qlast, p + 1)
                    pe.wait_ge(s_kT, 4 * p + 4)
                    for n in range(TILES * GROUPS):
                        t, g = n // GROUPS, n % GROUPS
                        if n >= 2:
                            pe.wait_ge(s_mx, TILES * GROUPS * p + n - 1)
                        for c in range(4):
                            u, j = 2 * g + c // 2, c % 2
                            rows = slice(HALF * j, HALF * j + SHIFT)
                            last = nc.tensor.matmul(psum[:, 2 * (n % 2) + j, (c // 2) * SEQ:(c // 2 + 1) * SEQ],
                                                    qT[rows, u, t * P:(t + 1) * P], kT[rows, u, :],
                                                    start=True, stop=True)
                        last.then_inc(s_ms, 1)
                    pe.wait_ge(s_mx, TILES * GROUPS * (p + 1))
                    for t in range(TILES):
                        last = nc.tensor.transpose(psum[0:NH, 4, t * P:(t + 1) * P], neg_max[:, t, :], ident[:, :])
                    last.then_inc(s_mT, 1)
                    pe.wait_ge(s_md, 32 * (p + 1))
                    scores(p, 0)
                    scores(p, 1)
                with pe.Else():
                    scores(p, 0)
                    scores(p, 1)
                    finish()
                if more:
                    pe.wait_ge(s_kT, 4 * p + 4)
                    pe.wait_ge(s_qlast, p + 1)
                    ln_transpose(0, p + 1, 0)
                    ln_transpose(0, p + 1, 1)
                for g in range(GROUPS):
                    if g < GROUPS - 1:
                        scores(p, 2 * g + 2)
                        if g == 1 and more:
                            pe.wait_ge(s_xv[0], 3 * p + 4)
                            ln_transpose(0, p + 1, 2)
                        if g == 0 and older:
                            pe.wait_ge(s_yg, (p - 1) * TILES)
                        scores(p, 2 * g + 3)
                    if more and g == GROUPS - 1:
                        pe.wait_ge(s_xv[0], 3 * p + 6)
                        pe.wait_ge(s_exp, UNITS * p + UNITS - 1)
                        qkv(p + 1, 0, (2,))
                    values(p, g)
                if more:
                    qkv(p + 1, 0, (0,))
                else:
                    pe.wait_ge(s_xs[1], 3 * p)
                    up(p - 1, 0)
                pe.wait_ge(s_attn, GROUPS * p + GROUPS)
                for t in range(TILES):
                    for g in range(GROUPS):
                        last = nc.tensor.transpose(psum[:, 6 + t, g * P:(g + 1) * P],
                                                   attn[:, g, t * P:(t + 1) * P], ident[:, :])
                    last.then_inc(s_oT, 1)
                if more:
                    qkv(p + 1, 0, (1,))
                    qkv(p + 1, 1, (2, 0))
                if not prev:
                    pe.wait_ge(s_wproj, 1)
                if not more:
                    up(p - 1, 1)
                o_back(p, 0)
                if more:
                    qkv(p + 1, 1, (1,))
                o_back(p, 1)
                if not prev:
                    project(p, 0)
                    project(p, 1)

                def between():
                    project(p, 0)
                    project(p, 1)
                    if more:
                        pe.wait_ge(s_v, (p + 1) * TILES + TILES)

                def behind(i):
                    if more:
                        if i == 0:
                            pe.wait_ge(s_pg, (p + 1) * TILES)
                        stack_transpose(p + 1, i)
                    if i == 2:
                        if more:
                            pe.wait_ge(s_qkn, (p + 1) * TILES + TILES)
                            pe.wait_ge(s_v, (p + 1) * TILES + TILES)
                        if prev:
                            pe.wait_ge(s_gelu, MU * (p - 1) + 4)
                        for j in range(3):
                            ln_transpose(1, p, j)

                if prev:
                    if more:
                        pe.wait_ge(s_v, (p + 1) * TILES + 1)
                    mlp(p - 1, (s_qkn, (p + 1) * TILES + 1) if more else None, between, behind, not more)
                else:
                    for i in range(MU - 1):
                        behind(i)
                if not prev:
                    pe.wait_ge(s_w1, 1)
                    pe.wait_ge(s_w1tail, 1)
                    pe.wait_ge(s_w2, 1)

            passes(pe, body)
            down(SEQS - 2, MU - 1)
            mlp(SEQS - 1, (s_yg, (SEQS - 1) * TILES), lambda: None, lambda i: None)
            down(SEQS - 1, MU - 1)

        @block.scalar
        def _(act):
            act.wait_ge(s_cond, 16)
            nc.scalar.activation(cond_tanh[:, :, :], cond[:, :, :], ACT.Tanh, scale=0.5).then_inc(s_tanh, 1)

            def modulate(which, n, j):
                xv = (xv_qkv, xv_mlp)[which]
                rows = P if j < 2 else TAIL3
                act.wait_ge(s_zT[which], 3 * n + j + 1)
                act.wait_ge(s_modc[which], n + 1)
                act.wait_ge(s_xs[which], 3 * n)
                dsts = [xv[0:rows, j, :]]
                if which == 0:
                    act.wait_ge(s_qkv, TILES * n)
                    dsts.append(xs_hi[0][:, j, :] if j < 2 else xs_tail[0][0:TAIL3, :])
                for dst in dsts:
                    last = nc.scalar.activation(dst, psum[0:rows, ln_bank(which, n)[j], 0:SEQ], ACT.Identity,
                                                bias=mod_cur[which][0:rows, 0, j:j + 1],
                                                scale=mod_cur[which][0:rows, 1, j:j + 1])
                last.then_inc(s_xv[which], 1)

            def qkv_read(q, t):
                act.wait_ge(s_qkv, q * TILES + t + 1)
                act.wait_ge(s_qsum, q * TILES)
                nc.scalar.activation(squares[:, t, :].rearrange("p (c n) -> p c n", c=2),
                                     psum[:, 3 * t:3 * t + 2, 0:H], ACT.Square).then_inc(s_sq, 1)
                act.wait_ge(s_pv, q * GROUPS)
                nc.scalar.activation(v_ext[:, t, :, 0:HD], psum[:, 3 * t + 2, 0:H].rearrange("p (h d) -> p h d", d=HD),
                                     ACT.Copy).then_inc(s_v, 1)

            def qk_high(q, t):
                n = q * TILES + t
                act.wait_ge(s_qkn, n + 1)
                act.wait_ge(s_stk, 4 * q)
                for c, src, places in ((1, qk_norm[:, t, H:QK], slice(0, 2)), (0, q_gained[:, t, :], slice(0, 3, 2))):
                    if c == 0:
                        act.wait_ge(s_qg, n + 1)
                    nc.scalar.activation(qk_stack[:, t, c, :, 0:SHIFT].rearrange("p h (r d) -> p h r d", r=3)[:, :, places, :],
                                         src.rearrange("p (h o d) -> p h o d", o=1, d=HD).broadcast_to((P, NH, 2, HD)),
                                         ACT.Copy).then_inc(s_qround, 1)

            def q_read(q, n):
                t, i = n // 2, n % 2
                act.wait_ge(s_stq, 4 * q + n + 1)
                act.wait_ge(s_score, UNITS * q)
                nc.scalar.activation(qT[:, 4 * i:4 * i + 4, t * P:(t + 1) * P],
                                     psum[:, 6, :].rearrange("p (u n) -> p u n", u=4), ACT.Copy).then_inc(s_qT, 1)

            def load_table(function):
                nc.scalar.activation(table_out[:, :], table_in[:, :], function)

            def exp(p, u):
                act.wait_ge(s_score, UNITS * p + u + 1)
                act.wait_ge(s_pv, GROUPS * p + u // 2 - 1 if u >= 4 else GROUPS * p)
                nc.scalar.activation(prob[:, u % 4, :].rearrange("p (c n) -> p c n", c=2),
                                     psum[:, score_bank(u):score_bank(u) + 2, :], ACT.Exp).then_inc(s_exp, 1)

            def o_read(p, t):
                act.wait_ge(s_oback, p * TILES + t + 1)
                act.wait_ge(s_proj, p * TILES)
                nc.scalar.activation(o_stack[:, t, :], psum[:, 6, :], ACT.Copy).then_inc(s_ostack, 1)
                nc.scalar.activation(o_tail[0:TAIL3, t * P:(t + 1) * P], psum[0:TAIL3, 7, 0:P], ACT.Copy).then_inc(s_ostack, 1)

            def gelu(m, i):
                n = SEQ * len(range(2 * i, min(2 * i + 2, FT)))
                act.wait_ge(s_up, MU * m + i + 1)
                act.wait_ge(s_hs, MU * m + i - 1 if i >= 2 else MU * m)
                act.wait_ge(s_down, MU * m + i - 1 if i >= 2 else MU * m)
                for dst in (hidden, hid_hi):
                    last = nc.scalar.activation(dst[:, i % 2, 0:n], psum[:, hidden_bank[i % 2], 0:n], ACT.Gelu_apprx_tanh)
                last.then_inc(s_gelu, 1)

            def round_weights(c, n, s_raw, s_hi):
                cols = slice(c, c + n)
                act.wait_ge(s_raw, 96)
                nc.scalar.activation(w_hi[:, :, cols], raw_w[:, 0:2, cols], ACT.Copy)
                nc.scalar.activation(w_tail[0:TAIL3 + 1, cols], raw_w[0:TAIL3 + 1, 2, cols], ACT.Copy).then_inc(s_hi, 1)

            act.wait_ge(s_bias0, 1)
            round_weights(W_PROJ, H, s_projraw, s_projhi)
            act.wait_ge(s_centred, 1)
            round_weights(W_QKV, 3 * H, s_qkvraw, s_qkvhi)
            round_weights(W_1, MLP, s_w1raw, s_w1hi)
            act.wait_ge(s_w2raw, 48)
            act.wait_ge(s_const, 2)
            nc.scalar.activation(w2_hi[:, :, :], raw_w2, ACT.Copy)
            nc.scalar.activation(b2_rows[0:1, :], gate2[0:1, :], ACT.Copy).then_inc(s_w2hi, 1)
            qkv_read(0, 0)
            qkv_read(0, 1)
            qk_high(0, 0)
            act.wait_ge(s_gatemm, 1)
            nc.scalar.activation(gate_rows[:, :, :], psum[0:SEQS, 6:8, 0:H], ACT.Copy).then_inc(s_gate, 1)
            q_read(0, 0)
            qk_high(0, 1)
            q_read(0, 1)
            q_read(0, 2)
            for s in (s_wproj, s_w1, s_w1tail, s_w2):
                act.wait_ge(s, 1)

            def body(p, further, more, prev, older):
                for u in range(UNITS):
                    exp(p, u)
                if more:
                    qkv_read(p + 1, 0)
                o_read(p, 0)
                o_read(p, 1)
                if more:
                    qkv_read(p + 1, 1)
                if prev:
                    load_table(ACT.Gelu_apprx_tanh)
                    gelu(p - 1, 0)
                if more:
                    qk_high(p + 1, 0)
                if prev:
                    gelu(p - 1, 1)
                if prev:
                    gelu(p - 1, 2)
                if more:
                    q_read(p + 1, 0)
                    qk_high(p + 1, 1)
                if prev:
                    gelu(p - 1, 3)
                if more:
                    q_read(p + 1, 1)
                if prev:
                    gelu(p - 1, 4)
                if more:
                    q_read(p + 1, 2)
                for j in range(3):
                    modulate(1, p, j)
                if more:
                    load_table(ACT.Exp)

            passes(act, body)
            for i in range(MU):
                gelu(SEQS - 1, i)

        @block.vector
        def _(dve):
            done = 0

            def step(ins):
                nonlocal done
                done += 1
                ins.then_inc(s_setup, 1)

            def ln_statistics(which, n, src):
                for t in range(TILES):
                    last = nc.vector.bn_stats(ln_stats[which][:, t, :], src[:, t, :])
                last.then_inc(s_stats[which], 1)

            def ln_variance(*of):
                for which, n in of:
                    dve.wait_ge(s_gain, 1)
                    dve.wait_ge(s_stats[which], n + 1)
                    for t in range(TILES):
                        last = nc.vector.bn_aggr(ln_mv[which][:, t, :], ln_stats[which][:, t, :])
                    last.then_inc(s_aggr[which], 1)
                for which, n in of:
                    dve.wait_ge(s_aggr[which], n + 1)
                    nc.vector.tensor_scalar_add(ln_var[which][:, :], ln_mv[which][:, :, 1], EPS).then_inc(s_var[which], 1)

            def normalise(which, n, src):
                dve.wait_ge(s_rstd[which], n + 1)
                for t in range(TILES):
                    args = (ln_mv[which][:, t, 0:1], ln_rstd[which][:, t:t + 1], ALU.subtract, ALU.mult)
                    nc.vector.tensor_scalar(z[:, t, 0:H], src[:, t, :], *args)
                    last = nc.vector.tensor_scalar(
                        z[:, t, H:ZW].rearrange("p (r n) -> p r n", r=2),
                        src[:, t, 2 * P:H].rearrange("p (o n) -> p o n", o=1).broadcast_to((P, 2, TAIL)), *args)
                last.then_inc(s_z[which], 1)

            def modulate(n, j):
                rows = P if j < 2 else TAIL3
                dve.wait_ge(s_modc[0], n + 1)
                dve.wait_ge(s_zT[0], 3 * n + j + 1)
                dve.wait_ge(s_xs[0], 3 * n)
                dve.wait_ge(s_qkv, TILES * n)
                high = xs_hi[0][:, j, :] if j < 2 else xs_tail[0][0:TAIL3, :]
                for dst in (xv_qkv[0:rows, j, :], high):
                    last = nc.vector.tensor_scalar(dst, psum[0:rows, ln_bank(0, n)[j], 0:SEQ],
                                                   mod_cur[0][0:rows, 1, j:j + 1], mod_cur[0][0:rows, 0, j:j + 1],
                                                   ALU.mult, ALU.add)
                last.then_inc(s_xv[0], 1)

            def round_x2(m):
                dve.wait_ge(s_xv[1], 3 * m + 3)
                dve.wait_ge(s_up, MU * m)
                nc.vector.tensor_copy(xs_hi[1][:, :, :], xv_mlp[:, 0:2, :])
                nc.vector.tensor_copy(xs_tail[1][0:TAIL3, :], xv_mlp[0:TAIL3, 2, :]).then_inc(s_x2round, 1)

            def split_x(which, n, j):
                xv, hi, lo, tail = (xv_qkv, xv_mlp)[which], xs_hi[which], xs_lo[which], xs_tail[which]
                if which == 0:
                    dve.wait_ge(s_xv[0], 3 * n + j + 1)
                else:
                    dve.wait_ge(s_x2round, n + 1)
                if j < 2:
                    nc.vector.tensor_tensor(lo[:, j, :], xv[:, j, :], hi[:, j, :], ALU.subtract).then_inc(s_xs[which], 1)
                else:
                    low = slice(TAIL, 2 * TAIL)
                    nc.vector.tensor_tensor(tail[low, :], xv[low, 2, :], tail[low, :], ALU.subtract).then_inc(s_xs[which], 1)

            def split_x2(m):
                for j in range(3):
                    split_x(1, m, j)

            def heads(ap):
                return ap.rearrange("p (h d) -> p h d", d=HD)

            def qk_variance(q, t):
                n = q * TILES + t
                dve.wait_ge(s_qvar, n)
                dve.wait_ge(s_sq, n + 1)
                nc.vector.tensor_reduce(qk_sum[:, :], heads(squares[:, t, :]), AX.X, ALU.add).then_inc(s_qsum, 1)
                dve.wait_ge(s_qsum, n + 1)
                if not isinstance(q, int) or q > 1:
                    dve.wait_ge(s_qrstd, q - 1)
                nc.vector.tensor_scalar(qk_var[:, t, :], qk_sum[:, :], 1.0 / HD, EPS, ALU.mult, ALU.add).then_inc(s_qvar, 1)

            def newton_before(q, t):
                return (t if isinstance(q, int) and q == 0 else q + 1) * RSQRT_STEPS_V

            def qk_rsqrt(q, t, meanwhile=None):
                var, r = qk_var[:, t, :], qk_rstd[:, t, :]
                dve.wait_ge(s_qvar, q * TILES + t + 1)
                nc.vector.tensor_scalar(r.bitcast(I32), var.bitcast(I32), -0.5, RSQRT_MAGIC, ALU.mult, ALU.add)
                nc.vector.tensor_scalar(half_v[:, :], var, -0.5, None, ALU.mult).then_inc(s_newton_v, 1)
                for i in range(3):
                    if i == 1 and meanwhile:
                        meanwhile()
                    steps = newton_before(q, t) + 3 * i
                    dve.wait_ge(s_newton_v, steps + 1)
                    nc.vector.tensor_tensor(square_v[:, :], r, r, ALU.mult).then_inc(s_newton_v, 1)
                    dve.wait_ge(s_newton_v, steps + 2)
                    nc.vector.tensor_tensor(square_v[:, :], square_v[:, :], half_v[:, :], ALU.mult).then_inc(s_newton_v, 1)
                    dve.wait_ge(s_newton_v, steps + 3)
                    nc.vector.scalar_tensor_tensor(r, square_v[:, :], 1.5, r, ALU.add, ALU.mult).then_inc(s_newton_v, 1)

            def qk_normalise(q, t):
                n = q * TILES + t
                if t == 0 or isinstance(q, int) and q == 0:
                    dve.wait_ge(s_newton_v, newton_before(q, t) + RSQRT_STEPS_V)
                else:
                    dve.wait_ge(s_qrstd, q)
                dve.wait_ge(s_stack, n - t)
                for c, s_done in ((1, None), (0, s_qkn)):
                    last = nc.vector.tensor_tensor(
                        heads(qk_norm[:, t, c * H:(c + 1) * H]), heads(psum[:, 3 * t + c, 0:H]),
                        qk_rstd[:, t, c * NH:(c + 1) * NH].rearrange("p (h o) -> p h o", o=1).broadcast_to((P, NH, HD)), ALU.mult)
                last.then_inc(s_qkn, 1)

            def qk_low(q, t):
                n = q * TILES + t
                dve.wait_ge(s_qround, 2 * n + 2)
                for c, low_at in ((1, 2 * HD), (0, HD)):
                    src = heads(qk_norm[:, t, H:QK] if c else q_gained[:, t, :])
                    last = nc.vector.tensor_tensor(qk_stack[:, t, c, :, low_at:low_at + HD], src,
                                                   qk_stack[:, t, c, :, 0:HD], ALU.subtract)
                last.then_inc(s_stack, 1)

            def k_read(q, n):
                t, i = n // 2, n % 2
                dve.wait_ge(s_stk, 4 * q + n + 1)
                dve.wait_ge(s_score, UNITS * q)
                nc.vector.tensor_copy(kT[:, 4 * i:4 * i + 4, t * P:(t + 1) * P],
                                      psum[:, 7, :].rearrange("p (u n) -> p u n", u=4)).then_inc(s_kT, 1)

            def last_q_read(q):
                dve.wait_ge(s_stq, 4 * q + 4)
                dve.wait_ge(s_score, UNITS * q)
                nc.vector.tensor_copy(qT[:, 4:8, P:2 * P], psum[:, 6, :].rearrange("p (u n) -> p u n", u=4)).then_inc(s_qlast, 1)

            def hand_on(m):
                dve.wait_ge(s_x2, m * TILES + TILES)
                dve.wait_ge(s_y, m * TILES)
                nc.vector.tensor_copy(x2_prev, x2).then_inc(s_x2c, 1)

            def attn_read(p, g):
                dve.wait_ge(s_pv, GROUPS * p + g + 1)
                dve.wait_ge(s_oT, p * TILES)
                nc.vector.tensor_copy(attn[:, g, :], psum[:, 4 + g % 2, 0:SEQ]).then_inc(s_attn, 1)

            def o_normalise(p, t):
                n = p * TILES + t
                of_head = psum[:, 6 + t, :].rearrange("p (h d) -> p h d", d=VW)
                dve.wait_ge(s_oT, n + 1)
                nc.vector.reciprocal(o_recip[:, :], of_head[:, :, HD]).then_inc(s_recip, 1)
                dve.wait_ge(s_recip, n + 1)
                nc.vector.tensor_tensor(heads(o_norm[:, t, :]), of_head[:, :, 0:HD],
                                        o_recip[:, :].rearrange("p (h o) -> p h o", o=1).broadcast_to((P, NH, HD)),
                                        ALU.mult).then_inc(s_on, 1)

            def o_split_tile(p, t):
                n = p * TILES + t
                dve.wait_ge(s_on, n + 1)
                dve.wait_ge(s_oback, p * TILES)
                nc.vector.tensor_copy(o_split[:, t, 0:H], o_norm[:, t, :])
                nc.vector.tensor_copy(o_split[:, t, H + TAIL:ZW], o_norm[:, t, 2 * P:H]).then_inc(s_oround, 1)
                dve.wait_ge(s_oround, n + 1)
                nc.vector.tensor_tensor(o_split[:, t, ZW:OW], o_norm[:, t, 0:2 * P], o_split[:, t, 0:2 * P], ALU.subtract)
                nc.vector.tensor_tensor(o_split[:, t, H:H + TAIL], o_norm[:, t, 2 * P:H], o_split[:, t, 2 * P:H],
                                        ALU.subtract).then_inc(s_os, 1)

            def residual(p, t):
                n = p * TILES + t
                dve.wait_ge(s_proj, n + 1)
                dve.wait_ge(s_g1, 16 * (p + 1))
                dve.wait_ge(s_x2c, p)
                nc.vector.tensor_tensor(x2[:, t, :], psum[:, 6 + t, 0:H], gate1[:, 0, :], ALU.mult).then_inc(s_pg, 1)
                dve.wait_ge(s_pg, n + 1)
                dve.wait_ge(s_xres, 16 * (p + 1))
                nc.vector.tensor_tensor(x2[:, t, :], x2[:, t, :], x_res[:, t, :], ALU.add).then_inc(s_x2, 1)

            def split_hidden(m, i):
                n = SEQ * len(range(2 * i, min(2 * i + 2, FT)))
                dve.wait_ge(s_gelu, MU * m + i + 1)
                dve.wait_ge(s_down, MU * m + i - 1 if i >= 2 else MU * m)
                nc.vector.tensor_tensor(hid_lo[:, i % 2, 0:n], hidden[:, i % 2, 0:n], hid_hi[:, i % 2, 0:n],
                                        ALU.subtract).then_inc(s_hs, 1)

            def gate_y(m):
                dve.wait_ge(s_down, MU * m + MU)
                dve.wait_ge(s_g2, 16 * (m + 1))
                dve.wait_ge(s_out, 16 * m)
                for t in range(TILES):
                    nc.vector.tensor_tensor(y[:, t, :], psum[:, t, 0:H], gate2[:, :], ALU.mult).then_inc(s_yg, 1)

            def finish_y(m):
                dve.wait_ge(s_x2c, m + 1)
                for t in range(TILES):
                    dve.wait_ge(s_yg, m * TILES + t + 1)
                    nc.vector.tensor_tensor(y[:, t, :], y[:, t, :], x2_prev[:, t, :], ALU.add).then_inc(s_y, 1)

            nc.vector.memset(w_tail[TAIL3:STACK, :].bitcast(F32), 0.0).then_inc(s_bias0, 1)
            for t in range(TILES):
                nc.vector.memset(qk_stack[:, t, :, :, SHIFT:HALF].bitcast(F32), 0.0)
            nc.vector.memset(v_ext[:, :, :, HD:VW], 0.0)
            nc.vector.memset(mod_all[:, :, :, :], 0.0)
            nc.vector.memset(b2_rows[:, :].bitcast(F32), 0.0)
            nc.vector.memset(ones_r[:, :].bitcast(F32), 1.0)
            nc.vector.memset(table_in[:, :], 0.0)
            for tail in (*xs_tail, o_tail):
                nc.vector.memset(tail[TAIL3:STACK, :].bitcast(F32), 1.0)
            step(nc.vector.memset(silu[KM:KM + 1, :, :], 1.0))
            dve.wait_ge(s_setup, done)
            nc.vector.memset(qk_stack[:, :, 1, :, SHIFT:SROWS].bitcast(F32), 1.0)
            nc.vector.memset(v_ext[:, :, :, HD:HD + 1], 1.0)
            dve.wait_ge(s_ident, 1)
            nc.vector.tensor_copy(ident_r[:, :], ident[:, :]).then_inc(s_const, 1)
            dve.wait_ge(s_tanh, 1)
            step(nc.vector.tensor_scalar(cond_tanh[:, :, :], cond_tanh[:, :, :], 0.5, 0.5, ALU.mult, ALU.add))
            dve.wait_ge(s_setup, done)
            nc.vector.tensor_tensor(silu[0:KM, :, :], cond_tanh[:, :, :], cond[:, :, :], ALU.mult).then_inc(s_silu, 1)
            dve.wait_ge(s_g, 32)
            step(nc.vector.tensor_tensor(gain[:, :], g_both[:, 0, :], g_both[:, 1, :], ALU.mult))
            dve.wait_ge(s_setup, done)
            step(nc.vector.tensor_scalar(gain[:, :], gain[:, :], HD ** -0.5, None, ALU.mult))
            dve.wait_ge(s_setup, done)
            nc.vector.tensor_reduce(bound[:, :], gain[:, :], AX.X, ALU.max, apply_absolute_value=True).then_inc(s_gain, 1)
            dve.wait_ge(s_gain, 1)
            nc.vector.tensor_scalar(flag[:, :], bound[:, :], float(HD), SCORE_BOUND, ALU.mult, ALU.is_gt).then_inc(s_flag, 1)
            dve.wait_ge(s_x, 16)
            ln_statistics(0, 0, x_ln)
            ln_variance((0, 0))
            normalise(0, 0, x_ln)
            dve.wait_ge(s_qkvraw, 96)
            rows_of = (P, P, STACK)
            for k, rows in enumerate(rows_of):
                nc.vector.tensor_reduce(col_mean[0:rows, k, :], heads(raw_w[0:rows, k, 0:QK]), AX.X, ALU.add)
            step(nc.vector.memset(bound[:, :], 0.0))
            dve.wait_ge(s_setup, done)
            for k, rows in enumerate(rows_of):
                last = nc.vector.tensor_scalar(col_mean[0:rows, k, :], col_mean[0:rows, k, :], 1.0 / HD, None, ALU.mult)
            step(last)
            dve.wait_ge(s_setup, done)
            for k, rows in enumerate(rows_of):
                last = nc.vector.tensor_tensor(
                    heads(raw_w[0:rows, k, 0:QK]), heads(raw_w[0:rows, k, 0:QK]),
                    col_mean[0:rows, k, :].rearrange("p (h o) -> p h o", o=1).broadcast_to((rows, 2 * NH, HD)), ALU.subtract)
            last.then_inc(s_centred, 1)
            def mod_read(which):
                dve.wait_ge(s_modmm, which + 1)
                cols = psum[:, mod_bank[which], 0:6 * SEQS].rearrange("p (k j b) -> p k j b", k=2, j=3)
                for rows, j in ((P, slice(0, 2)), (TAIL3, slice(2, 3))):
                    nc.vector.tensor_copy(mod_all[0:rows, 2 * which, j, :], cols[0:rows, 0, j, :])
                    last = nc.vector.tensor_scalar_add(mod_all[0:rows, 2 * which + 1, j, :], cols[0:rows, 1, j, :], 1.0)
                last.then_inc(s_mod, 1)

            mod_read(0)
            dve.wait_ge(s_mod, 1)
            nc.vector.tensor_copy(mod_cur[0][:, :, :], mod_all[:, 0:2, :, 0]).then_inc(s_modc[0], 1)
            for j in range(3):
                modulate(0, j)
            for j in range(3):
                split_x(0, 0, j)
            dve.wait_ge(s_qkvhi, 1)
            low = slice(2 * TAIL, STACK)
            nc.vector.tensor_tensor(w_tail[low, 0:3 * H], raw_w[low, 2, 0:3 * H], w_tail[low, 0:3 * H], ALU.subtract)
            nc.vector.tensor_tensor(w_lo[:, :, 0:3 * H], raw_w[:, 0:2, 0:3 * H], w_hi[:, :, 0:3 * H], ALU.subtract).then_inc(s_wqkv, 1)
            mod_read(1)
            dve.wait_ge(s_w1hi, 1)
            cols = slice(W_1, W_1 + MLP)
            nc.vector.tensor_tensor(w_tail[low, cols], raw_w[low, 2, cols], w_tail[low, cols], ALU.subtract).then_inc(s_w1tail, 1)
            dve.wait_ge(s_w2hi, 1)
            nc.vector.tensor_tensor(w2_lo[:, :, :], raw_w2, w2_hi[:, :, :], ALU.subtract)
            nc.vector.tensor_tensor(b2_rows[0:2, :], gate2[0:2, :], b2_rows[0:2, :], ALU.subtract).then_inc(s_w2, 1)
            qk_variance(0, 0)
            qk_rsqrt(0, 0)
            qk_normalise(0, 0)
            qk_variance(0, 1)
            qk_rsqrt(0, 1, lambda: qk_low(0, 0))
            qk_normalise(0, 1)
            k_read(0, 0)
            dve.wait_ge(s_x, 32)
            ln_statistics(0, 1, x_ln)
            qk_low(0, 1)
            ln_variance((0, 1))
            k_read(0, 1)
            k_read(0, 2)
            normalise(0, 1, x_ln)
            last_q_read(0)
            k_read(0, 3)
            for s in (s_wproj, s_w1):
                dve.wait_ge(s, 1)
            needs_shift = dve.value_load(flag[0:1, 0:1], min_val=0, max_val=1)

            def body(p, further, more, prev, older):
                if older:
                    gate_y(p - 2)
                with dve.If(needs_shift > 0):
                    for n in range(TILES * GROUPS):
                        t, g = n // GROUPS, n % GROUPS
                        dve.wait_ge(s_ms, TILES * GROUPS * p + n + 1)
                        two = 2 * (n % 2)
                        nc.vector.tensor_reduce(
                            neg_max[:, t, :].rearrange("p (j u) -> p j u", j=2)[:, :, 2 * g:2 * g + 2],
                            psum[:, two:two + 2, :].rearrange("p j (u n) -> p j u n", u=2),
                            AX.X, ALU.max, negate=True).then_inc(s_mx, 1)
                    dve.wait_ge(s_mT, p + 1)
                    dve.wait_ge(s_md, 32 * p)
                    nc.vector.tensor_copy(shiftT[:, :], psum[0:NH, 4, 0:SEQ]).then_inc(s_mc, 1)
                if more:
                    modulate(p + 1, 0)
                    modulate(p + 1, 1)
                attn_read(p, 0)
                if more:
                    split_x(0, p + 1, 0)
                    split_x(0, p + 1, 1)
                    modulate(p + 1, 2)
                attn_read(p, 1)
                if more:
                    split_x(0, p + 1, 2)
                if older:
                    finish_y(p - 2)
                if prev:
                    round_x2(p - 1)
                attn_read(p, 2)
                if prev:
                    hand_on(p - 1)
                    split_x2(p - 1)
                attn_read(p, 3)
                for t in range(TILES):
                    o_normalise(p, t)
                    o_split_tile(p, t)
                if more:
                    qk_variance(p + 1, 0)
                    qk_rsqrt(p + 1, 0)
                    qk_normalise(p + 1, 0)
                    qk_variance(p + 1, 1)
                if prev:
                    split_hidden(p - 1, 0)
                residual(p, 0)
                residual(p, 1)
                if more:
                    qk_low(p + 1, 0)
                if prev:
                    split_hidden(p - 1, 1)
                if further:
                    dve.wait_ge(s_x, 16 * (p + 3))
                    ln_statistics(0, p + 2, x_ln)
                if more:
                    qk_normalise(p + 1, 1)
                dve.wait_ge(s_x2, p * TILES + TILES)
                ln_statistics(1, p, x2)
                ln_variance(*([(0, p + 2)] if further else []), (1, p))
                if prev:
                    split_hidden(p - 1, 2)
                if more:
                    k_read(p + 1, 0)
                    qk_low(p + 1, 1)
                    dve.wait_ge(s_zT[0], 3 * (p + 2))
                else:
                    dve.wait_ge(s_zT[0], 3 * (p + 1))
                normalise(1, p, x2)
                if more:
                    k_read(p + 1, 1)
                if prev:
                    split_hidden(p - 1, 3)
                if prev:
                    split_hidden(p - 1, 4)
                if more:
                    k_read(p + 1, 2)
                if further:
                    dve.wait_ge(s_zT[1], 3 * (p + 1))
                    normalise(0, p + 2, x_ln)
                if more:
                    last_q_read(p + 1)
                    k_read(p + 1, 3)

            passes(dve, body)
            last = SEQS - 1
            round_x2(last)
            split_x2(last)
            gate_y(last - 1)
            finish_y(last - 1)
            hand_on(last)
            for i in range(MU):
                split_hidden(last, i)
            gate_y(last)
            finish_y(last)


def kernel(x, cond_1152, L0_cond_w_mod, L0_cond_b_mod, L0_cond_w_qkv, L0_cond_b_qkv, L0_cond_g_q, L0_cond_g_k,
           L0_cond_w_proj, L0_cond_b_proj, L0_cond_w1, L0_cond_b1, L0_cond_w2, L0_cond_b2):
    import numpy as np
    from concourse import bacc
    from concourse.bass_utils import run_bass_kernel_spmd

    arrays = {"x": x, "condT": np.asarray(cond_1152).T, "w_mod": L0_cond_w_mod, "b_mod": L0_cond_b_mod,
              "w_qkv": L0_cond_w_qkv, "b_qkv": L0_cond_b_qkv, "g_q": L0_cond_g_q, "g_k": L0_cond_g_k,
              "w_proj": L0_cond_w_proj, "b_proj": L0_cond_b_proj, "w1": L0_cond_w1, "b1": L0_cond_b1,
              "w2": L0_cond_w2, "b2": L0_cond_b2}
    nc = bacc.Bacc("TRN2", target_bir_lowering=False, num_devices=1)
    feeds, args = {}, []
    for name, a in arrays.items():
        a = np.ascontiguousarray(a)
        feeds[f"in_{name}"] = a
        args.append(nc.dram_tensor(f"in_{name}", a.shape, mybir.dt.from_np(a.dtype), kind="ExternalInput").ap())
    args.append(nc.dram_tensor("gate_scratch", (SEQS, 2 * H), F32, kind="Internal").ap())
    args.append(nc.dram_tensor("out_0", x.shape, F32, kind="ExternalOutput").ap())
    dit_block(nc, *args)
    r = run_bass_kernel_spmd(nc, [feeds], core_ids=[0])
    return r.results[0]["out_0"]
```
